# Optimizing a Trainium2 kernel written in Bass

```python
import numpy as np
import jax
import jax.numpy as jnp

def _softmax(x, axis=-1):
    return jax.nn.softmax(x, axis=axis)

def _gelu(x):
    return jax.nn.gelu(x, approximate=True)

def _silu(x):
    return jax.nn.silu(x)

def _sigmoid(x):
    return jax.nn.sigmoid(x)

def _layernorm(x, axis=-1, eps=1e-05):
    m = jnp.mean(x, axis=axis, keepdims=True)
    v = jnp.var(x, axis=axis, keepdims=True)
    return (x - m) / jnp.sqrt(v + eps)

def _scatter_add(tgt, idx, src, axis=0):
    return tgt.at[idx].add(src)

def _segment_sum(src, seg, n):
    return jax.ops.segment_sum(src, seg, n)
kernel_name = 'mk_macaron_d1_jaxref_r4_5c053b'

def setup_inputs(seed: int=0):
    np.random.seed(seed)
    _w = jnp.asarray

    def _L0_attn_setup():
        import jax, jax.numpy as jnp
        import numpy as np
        from math import log2, floor
        HEADS = 16
        DIM_HEAD = 64
        SCALE = DIM_HEAD ** (-0.5)

        def _get_slopes(heads):

            def pow2_slopes(n):
                start = 2 ** (-2 ** (-(log2(n) - 3)))
                return [start * start ** i for i in range(n)]
            if log2(heads).is_integer():
                return pow2_slopes(heads)
            c = 2 ** floor(log2(heads))
            return pow2_slopes(c) + pow2_slopes(2 * c)[0::2][:heads - c]
        key = jax.random.key(seed)
        k1, k2, k3 = jax.random.split(key, 3)
        b, n, dim = (2, 512, 256)
        inner = HEADS * DIM_HEAD
        x = jax.random.normal(k1, (b, n, dim), dtype=jnp.float32)
        w_qkv = jax.random.normal(k2, (dim, 3 * inner), dtype=jnp.float32) * dim ** (-0.5)
        w_out = jax.random.normal(k3, (inner, dim), dtype=jnp.float32) * inner ** (-0.5)
        b_out = jnp.zeros((dim,), dtype=jnp.float32)
        return {'x': x, 'w_qkv': w_qkv, 'w_out': w_out, 'b_out': b_out}
    _L0_attn_in = _L0_attn_setup()

    def _L0_ffn_setup():
        import jax, jax.numpy as jnp
        import numpy as np
        N_EMBD = 256
        N_STATE = 1024
        key = jax.random.key(seed)
        k_x, k_w1, k_b1, k_w2, k_b2 = jax.random.split(key, 5)
        x = jax.random.normal(k_x, (4, 512, N_EMBD), dtype=jnp.float32)
        w1 = jax.random.normal(k_w1, (N_EMBD, N_STATE), dtype=jnp.float32) * (1.0 / np.sqrt(N_EMBD))
        b1 = jax.random.normal(k_b1, (N_STATE,), dtype=jnp.float32) * 0.02
        w2 = jax.random.normal(k_w2, (N_STATE, N_EMBD), dtype=jnp.float32) * (1.0 / np.sqrt(N_STATE))
        b2 = jax.random.normal(k_b2, (N_EMBD,), dtype=jnp.float32) * 0.02
        return {'x': x, 'w1': w1, 'b1': b1, 'w2': w2, 'b2': b2}
    _L0_ffn_in = _L0_ffn_setup()
    _d = {'L0_attn_x': _L0_attn_in['x'], 'L0_attn_w_qkv': _L0_attn_in['w_qkv'], 'L0_attn_w_out': _L0_attn_in['w_out'], 'L0_attn_b_out': _L0_attn_in['b_out'], 'L0_ffn_w1': _L0_ffn_in['w1'], 'L0_ffn_b1': _L0_ffn_in['b1'], 'L0_ffn_w2': _L0_ffn_in['w2'], 'L0_ffn_b2': _L0_ffn_in['b2']}
    _x0 = _d['L0_attn_x']
    _d['L0_attn_x'] = jax.random.normal(jax.random.fold_in(jax.random.key(seed), 1), (16, 512, 256), dtype=_x0.dtype)
    del _x0
    return _d

def reference(L0_attn_x, L0_attn_w_qkv, L0_attn_w_out, L0_attn_b_out, L0_ffn_w1, L0_ffn_b1, L0_ffn_w2, L0_ffn_b2):

    def _L0_attn_ref(x, w_qkv, w_out, b_out):
        import jax, jax.numpy as jnp
        import numpy as np
        from math import log2, floor
        HEADS = 16
        DIM_HEAD = 64
        SCALE = DIM_HEAD ** (-0.5)

        def _get_slopes(heads):

            def pow2_slopes(n):
                start = 2 ** (-2 ** (-(log2(n) - 3)))
                return [start * start ** i for i in range(n)]
            if log2(heads).is_integer():
                return pow2_slopes(heads)
            c = 2 ** floor(log2(heads))
            return pow2_slopes(c) + pow2_slopes(2 * c)[0::2][:heads - c]
        b, n, _ = x.shape
        qkv = x @ w_qkv
        q, k, v = jnp.split(qkv, 3, axis=-1)

        def to_heads(t):
            return t.reshape(b, n, HEADS, DIM_HEAD).transpose(0, 2, 1, 3)
        q, k, v = map(to_heads, (q, k, v))
        q = q * SCALE
        sim = jnp.einsum('bhid,bhjd->bhij', q, k)
        slopes = jnp.asarray(_get_slopes(HEADS), dtype=sim.dtype)[:, None, None]
        i = jnp.arange(n)
        rel = -jnp.abs(i[None, :] - i[:, None]).astype(sim.dtype)
        sim = sim + rel[None, :, :] * slopes
        causal = jnp.triu(jnp.ones((n, n), dtype=bool), 1)
        mask_value = -jnp.finfo(sim.dtype).max
        sim = jnp.where(causal, mask_value, sim)
        attn = jax.nn.softmax(sim, axis=-1)
        out = jnp.einsum('bhij,bhjd->bhid', attn, v)
        out = out.transpose(0, 2, 1, 3).reshape(b, n, HEADS * DIM_HEAD)
        return out @ w_out + b_out

    def _L0_ffn_ref(x, w1, b1, w2, b2):
        import jax, jax.numpy as jnp
        import numpy as np
        N_EMBD = 256
        N_STATE = 1024
        h = jax.nn.gelu(jnp.einsum('bse,eh->bsh', x, w1) + b1, approximate=False)
        return jnp.einsum('bsh,he->bse', h, w2) + b2
    x = L0_attn_x
    x = x + 0.5 * _L0_ffn_ref(_layernorm(x, axis=-1), L0_ffn_w1, L0_ffn_b1, L0_ffn_w2, L0_ffn_b2)
    x = x + _L0_attn_ref(_layernorm(x, axis=-1), L0_attn_w_qkv, L0_attn_w_out, L0_attn_b_out)
    x = x + 0.5 * _L0_ffn_ref(_layernorm(x, axis=-1), L0_ffn_w1, L0_ffn_b1, L0_ffn_w2, L0_ffn_b2)
    return x

_drawn_inputs = setup_inputs


def setup_inputs(seed=0):
    import zlib

    import numpy as np

    out = dict(_drawn_inputs(seed))
    spreads = {'L0_attn_b_out': (0.0, 0.1)}
    factors = {'L0_ffn_b1': 4.925, 'L0_ffn_b2': 3.236}
    for name, (base, spread) in spreads.items():
        noise = np.random.default_rng([zlib.crc32(name.encode()), seed]).standard_normal(out[name].shape)
        drawn = base * np.exp(spread * noise) if base else spread * noise
        out[name] = jnp.asarray(drawn.astype(out[name].dtype))
    for name, factor in factors.items():
        out[name] = (out[name] * factor).astype(out[name].dtype)
    return out
```

```python
def build(nc, x_d, w_qkv_d, w_out_d, b_out_d, w1_d, b1_d, w2_d, b2_d, y_d):
    from concourse import mybir

    F32 = mybir.dt.float32
    F32R = mybir.dt.float32r
    I32 = mybir.dt.int32
    ALU = mybir.AluOpType
    ACT = mybir.ActivationFunctionType

    NB = x_d.shape[0]
    T, D, H, DH, F = 512, 256, 16, 64, 1024
    NT, NK, NM, NC = T // 128, D // 128, F // 128, H // 2
    EPS = 1e-5
    BIG = 3.0e38
    SLOPE = [2.0 ** (-0.5 * (h + 1)) for h in range(H)]
    BASE = {3: 0, 2: 512, 0: 896, 1: 1024}
    QBASE = BASE
    KBASE = {0: 0, 1: 512, 3: 896, 2: 1024}
    QORDER = (3, 2, 0, 1)
    PW = 1280

    at = [16512]

    def place(name, shape, dt, offset=None):
        n = 4
        for s in shape[1:]:
            n *= s
        if offset is None:
            offset = at[0]
            at[0] += -(-n // 32) * 32
        assert offset + n <= nc.sbuf_usable_end, name
        return nc.alloc_sbuf_tensor_at(name, list(shape), dt, offset=offset)

    w1h, w1l = place("w1h", [128, NK, F], F32R), place("w1l", [128, NK, F], F32R)
    w2h, w2l = place("w2h", [128, NM, D], F32R), place("w2l", [128, NM, D], F32R)
    wqh, wql = place("wqh", [128, NK, 3 * H * DH], F32R), place("wql", [128, NK, 3 * H * DH], F32R)
    woh, wol = place("woh", [128, NC, D], F32R), place("wol", [128, NC, D], F32R)
    dist = place("dist", [128, T], F32)
    ident = place("ident", [128, 128], F32)
    b2h = place("b2h", [128, D], F32)
    bo = place("bo", [128, D], F32)
    b1c = place("b1c", [128, NM], F32)
    mhalf = place("mhalf", [128, NT], F32)
    st = place("st", [128, 3, NT, 6], F32)
    mv = place("mv", [128, 3, NT, 2], F32)
    ve = place("ve", [128, 3, NT], F32)
    rstd = place("rstd", [128, 3, NT], F32)
    mx = place("mx", [128, 4, NT], F32)
    sm = place("sm", [128, 4, NT], F32)
    rs = place("rs", [128, 4, NT], F32)
    x0 = place("x0", [128, NT, D], F32)
    x1 = place("x1", [128, NT, D], F32)
    x2 = place("x2", [128, NT, D], F32)
    xn = place("xn", [128, 2, D], F32)
    xth, xtl = place("xth", [128, NK, T], F32R), place("xtl", [128, NK, T], F32R)
    o = place("o", [128, NC, T], F32)

    R = at[0]
    qk = place("qk", [128, 4, T], F32R, R)
    stack = [place(f"stack{i}", [128, 3, T], F32R, R + 8192 + 6144 * i) for i in range(2)]
    v = [place(f"v{i}", [128, NT, 4, 128], F32R, R + 20480 + 8192 * i) for i in range(2)]
    P = [place(f"P{i}", [128, PW], F32, R + 36864 + 4 * PW * i) for i in range(2)]
    pth = [place(f"pth{i}", [128, PW], F32R, R + 47104 + 8 * PW * i) for i in range(2)]
    ptl = [place(f"ptl{i}", [128, PW], F32R, R + 47104 + 4 * PW + 8 * PW * i) for i in range(2)]
    gh = place("gh", [128, NM, T], F32R, R + 34816)
    gl = place("gl", [128, NM, T], F32R, R + 34816 + 16384)
    oh = [place(f"oh{i}", [128, NC, 128], F32R, R + 8192 * i) for i in range(2)]
    ol = [place(f"ol{i}", [128, NC, 128], F32R, R + 4096 + 8192 * i) for i in range(2)]
    gt = place("gt", [128, 3, T], F32, R + 16384)
    raw1 = place("raw1", [128, NK, F], F32, R)
    raw2 = place("raw2", [128, NM, D], F32, R + 8192)
    rawo = place("rawo", [128, NC, D], F32, R + 16384)
    rawq = place("rawq", [128, NK, 3 * H * DH], F32, R + 24576)
    iota = place("iota", [128, T], I32, R + 49152)

    bank = [nc.alloc_psum_tensor(f"bank{i}", [128, 512], F32) for i in range(0)]
    psA = nc.alloc_psum_tensor("psA", [128, 3 * 512], F32)
    psB = nc.alloc_psum_tensor("psB", [128, 3 * 512], F32)
    psC = nc.alloc_psum_tensor("psC", [128, 512], F32)
    psD = nc.alloc_psum_tensor("psD", [128, 512], F32)

    def bk(i):
        if i < 3:
            return psA[:, 512 * i:512 * i + 512]
        if i < 6:
            return psB[:, 512 * (i - 3):512 * (i - 3) + 512]
        return (psC if i == 6 else psD)[:, :]

    B = range(NB)
    ffn = [(1, 0)] + [e for b in B for e in ([(1, b + 1)] if b + 1 < NB else []) + [(2, b)]]
    lns = [(1, 0), (2, 0)] + [e for b in B for e in (
        [(1, b + 1), (3, b), (2, b + 1)] if b + 1 < NB else [(3, b)])]

    def tiles_of(s):
        if s == -1:
            return [("q", 0), ("k", 0), ("v", 0, 0), ("v", 0, 1)]
        c, odd = divmod(s, 2)
        if odd:
            g, u = c // 2 + 1, c % 2
            return [("v", g, u)] if g < 4 else []
        return [("q", c + 1), ("k", c + 1)] if c + 1 < NC else []

    tiles = [t for s in range(-1, H) for t in tiles_of(s)]
    heads = [(b, h) for b in B for h in range(H)]
    per_block = [(b, h, i) for b, h in heads for i in QORDER]
    units = [(L, b, u) for L, b in lns for u in range(2)]
    rows = [(L, b, t) for L, b in lns for t in range(NT)]
    hidden = [(f, b, m) for f, b in ffn for m in range(NM)]
    down = [(f, b, t) for f, b in ffn for t in range(NT)]
    outs = [(b, t) for b in B for t in range(NT)]
    proj = [(b, t) for b in B for t in tiles]

    class Events:
        def __init__(self, name, keys, step=1):
            self.sem, self.step, self.made = nc.alloc_semaphore(name), step, 0
            self.keys = list(keys)
            self.value = {k: step * (n + 1) for n, k in enumerate(self.keys)}

        def by(self, instruction, key):
            assert self.keys[self.made] == key, (self.sem, key, self.keys[self.made])
            self.made += 1
            instruction.then_inc(self.sem, self.step)

        def wait(self, engine, key):
            engine.wait_ge(self.sem, self.value[key])

    e_qk = Events("qk_done", per_block)
    e_tp = Events("tp_done", heads)
    e_pv = Events("pv_done", heads)
    e_pj = Events("pj_done", proj)
    e_lt = Events("lt_done", units)
    e_up = Events("up_done", hidden)
    e_dn = Events("dn_done", down)
    e_ot = Events("ot_done", outs)
    e_ex = Events("ex_done", per_block)
    e_hp = Events("hp_done", heads)
    e_oc = Events("oc_done", heads)
    e_ph = Events("ph_done", proj)
    e_lh = Events("lh_done", units)
    e_gl = Events("gl_done", hidden)
    e_oh = Events("oh_done", outs)
    e_tt = Events("tt_done", per_block)
    e_rc = Events("rc_done", heads)
    e_lo = Events("lo_done", heads)
    e_oa = Events("oa_done", heads)
    e_pl = Events("pl_done", proj)
    e_ll = Events("ll_done", units)
    e_gh = Events("gh_done", hidden)
    e_gs = Events("gs_done", hidden)
    e_ol = Events("ol_done", outs)
    e_r1 = Events("r1_done", [(f, b, t) for f, b, t in down if f == 1])
    e_r3 = Events("r3_done", [(f, b, t) for f, b, t in down if f == 2])
    e_r2 = Events("r2_done", outs)
    e_bs = Events("bs_done", rows)
    e_ba = Events("ba_done", rows)
    ve_order = [(1, 0), (2, 0)] + [e for b in B for e in (
        [(1, b + 1), (3, b), (2, b + 1)] if b + 1 < NB else [(3, b)])]
    e_ve = Events("ve_done", ve_order)
    e_xn = Events("xn_done", rows)
    e_nz = Events("nz_done", per_block)
    e_pw = Events("pw_done", ve_order)
    e_pb = Events("pb_done", lns)
    e_x = Events("x_in", list(B), 16)
    e_y = Events("y_out", list(B), 16)
    e_sk = [Events(f"stack_in{i}", [(b, h, n) for b, h in heads if h % 2 == i for n in range(3)], 16)
            for i in range(2)]
    names = ["w1", "b1", "w2", "b2", "wqkv", "wout", "bout"]
    e_w = {n: Events("in_" + n, [0], 16) for n in names}
    e_sh = Events("set_hi", ["w1", "w2"] + [("q", h) for h in range(H)] + ["kv", "wout"])
    e_sl = Events("set_lo", ["w1", "w2"] + [("q", h) for h in range(H)] + ["kv", "wout"])
    e_sb = Events("set_bias", ["w2", "b2"])
    e_id = Events("set_ident", ["zero", "ident", "iota", "dist", "mhalf"])
    e_df = Events("set_dist", [0])

    SH = {"w1": (w1h, w1l, raw1), "w2": (w2h, w2l, raw2), "wout": (woh, wol, rawo)}

    def qcols(h):
        return slice(h * DH, (h + 1) * DH)

    HD = H * DH
    KV = slice(HD, 3 * HD)

    def q_scale(h):
        return DH ** -0.5 / SLOPE[h]

    block = nc.Block()
    with block:
        @block.sync
        def _(e):
            e_w_in = [
                ("w1", raw1[:, :, :], w1_d.rearrange("(k p) n -> p k n", p=128)),
                ("b1", b1c[:, :], b1_d.rearrange("(m p) -> p m", p=128)),
                ("w2", raw2[:, :, :], w2_d.rearrange("(m p) n -> p m n", p=128)),
                ("b2", b2h[:, :], b2_d.partition_broadcast(128)),
                ("wqkv", rawq[:, :, :], w_qkv_d.rearrange("(k p) n -> p k n", p=128)),
                ("wout", rawo[:, :, :], w_out_d.rearrange("(c p) n -> p c n", p=128)),
                ("bout", bo[:, :], b_out_d.partition_broadcast(128)),
            ]

            def load_x(b):
                if b > 0:
                    e_r1.wait(e, (1, b - 1, NT - 1))
                e_x.by(e.dma_start(x0[:, :, :], x_d[b].rearrange("(t p) n -> p t n", p=128)), b)

            load_x(0)
            for n, dst, src in e_w_in:
                e_w[n].by(e.dma_start(dst, src, allow_slow_non_contiguous=(n == "b1")), 0)

            def stack_head(b, h):
                c, i = h // 2, h % 2
                e_pl.wait(e, (b, ("k", c)))
                n = heads.index((b, h))
                if n >= 2:
                    e_qk.wait(e, (*heads[n - 2], QORDER[-1]))
                src = qk[64 * i:64 * i + 64, :, :].bitcast(F32)
                dst = stack[i]
                e_sk[i].by(e.dma_start(dst[0:64, :, :].bitcast(F32), src[:, 0:3, :]), (b, h, 0))
                e_sk[i].by(e.dma_start(dst[64:128, 1:3, :].bitcast(F32), src[:, 1:3, :]), (b, h, 1))
                e_sk[i].by(e.dma_start(dst[64:128, 0, :].bitcast(F32), src[:, 3, :]), (b, h, 2))

            for b in B:
                stack_head(b, 0)
                stack_head(b, 1)
                if b + 1 < NB:
                    load_x(b + 1)
                for h in range(2, H):
                    stack_head(b, h)
                e_r3.wait(e, (2, b, NT - 1))
                e_y.by(e.dma_start(y_d[b].rearrange("(t p) n -> p t n", p=128), x2[:, :, :]), b)
            e_y.wait(e, NB - 1)

        @block.tensor
        def _(e):
            def mm(out, lhsT, rhs, first, last):
                return e.matmul(out, lhsT, rhs, start=first, stop=last)

            def three(out, pairs):
                n = len(pairs)
                for i, (ah, al, bh, bl) in enumerate(pairs):
                    mm(out, ah, bh, i == 0, False)
                    mm(out, ah, bl, False, False)
                    inst = mm(out, al, bh, False, i == n - 1)
                return inst

            def ln_transpose(L, b, u):
                dst = bk(7) if L == 1 else bk(3 + u)
                n = units.index((L, b, u))
                if L == 1:
                    if u == 1:
                        e_ll.wait(e, (L, b, 0))
                    elif b > 0:
                        e_pl.wait(e, (b - 1, tiles[-1]))
                elif L == 3:
                    e_r2.wait(e, (b, 2 + u))
                elif b > 0:
                    e_ll.wait(e, (3, b - 1, u))
                for t in (2 * u, 2 * u + 1):
                    e_xn.wait(e, (L, b, t))
                    for k in range(NK):
                        col = k * 256 + (t - 2 * u) * 128
                        last = e.transpose(dst[:, col:col + 128], xn[:, t % 2, k * 128:(k + 1) * 128], ident[:, :])
                e_lt.by(last, (L, b, u))

            def up(f, b):
                L = 1 if f == 1 else 3
                e_ll.wait(e, (L, b, 1))
                if f == 1 and b > 0:
                    e_tt.wait(e, (b - 1, H - 1, QORDER[-1]))
                if f == 2 and b + 1 < NB:
                    e_gl.wait(e, (1, b + 1, NM - 1))
                if f == 2 and b + 1 == NB:
                    e_tt.wait(e, (b, H - 1, QORDER[-1]))
                for m in range(NM):
                    if m >= 3:
                        e_gl.wait(e, (f, b, m - 3))
                    ms = slice(m * 128, m * 128 + 128)
                    last = three(bk(m % 3), [(w1h[:, k, ms], w1l[:, k, ms], xth[:, k, :], xtl[:, k, :])
                                             for k in range(NK)])
                    e_up.by(last, (f, b, m))

            def dn(f, b, t):
                if t >= 2:
                    (e_r1 if f == 1 else e_r3).wait(e, (f, b, t - 2))
                elif f == 1 and b > 0:
                    e_lo.wait(e, (b - 1, H - 1))
                    e_oa.wait(e, (b - 1, H - 1))
                elif f == 2 and b + 1 < NB:
                    e_r1.wait(e, (1, b + 1, NT - 2 + t))
                elif f == 2:
                    e_lo.wait(e, (b, H - 1))
                    e_oa.wait(e, (b, H - 1))
                e_gs.wait(e, (f, b, NM - 1))
                ts = slice(t * 128, t * 128 + 128)
                last = three(bk(5 + t % 2)[:, 0:D], [(gh[:, m, ts], gl[:, m, ts], w2h[:, m, :], w2l[:, m, :])
                                                   for m in range(NM)])
                e_dn.by(last, (f, b, t))

            def out_proj(b, t):
                if t >= 2:
                    e_r2.wait(e, (b, t - 2))
                else:
                    e_lo.wait(e, (b, H - 1))
                e_ol.wait(e, (b, t))
                i = t % 2
                last = three(bk(3 + i)[:, 0:D], [(oh[i][:, c, :], ol[i][:, c, :], woh[:, c, :], wol[:, c, :])
                                               for c in range(NC)])
                e_ot.by(last, (b, t))

            def proj_tile(b, tile):
                n = proj.index((b, tile))
                if tile == tiles[0]:
                    e_ll.wait(e, (2, b, 1))
                    if b > 0:
                        e_ll.wait(e, (1, b, 1))
                if n > 0:
                    e_pl.wait(e, proj[n - 1])
                dst = bk(7)
                if tile[0] == "v":
                    _, g, u = tile
                    gs = slice(2 * HD + g * 256, 2 * HD + g * 256 + 256)
                    for j in range(2):
                        ts = slice((2 * u + j) * 128, (2 * u + j) * 128 + 128)
                        last = three(dst[:, j * 256:j * 256 + 256],
                                     [(xth[:, k, ts], xtl[:, k, ts], wqh[:, k, gs], wql[:, k, gs])
                                      for k in range(NK)])
                else:
                    kind, c = tile
                    cs = slice((HD if kind == "k" else 0) + c * 128, (HD if kind == "k" else 0) + c * 128 + 128)
                    last = three(dst, [(wqh[:, k, cs], wql[:, k, cs], xth[:, k, :], xtl[:, k, :])
                                       for k in range(NK)])
                e_pj.by(last, (b, tile))

            def scores(b, h):
                n = heads.index((b, h))
                sk = stack[h % 2]
                e_sk[h % 2].wait(e, (b, h, 2))
                if h == 0 and b > 0:
                    e_gl.wait(e, (2, b - 1, NM - 1))
                for i in QORDER:
                    if n > 0:
                        e_tt.wait(e, (*heads[n - 1], 0 if i == 2 else i))
                    w = 128 * (i + 1)
                    dst = psA[:, QBASE[i]:QBASE[i] + w]
                    qs = sk[:, 0, i * 128:i * 128 + 128]
                    mm(dst, qs, sk[:, 1, 0:w], True, False)
                    e_qk.by(mm(dst, qs, sk[:, 2, 0:w], False, True), (b, h, i))

            def transposes(b, h):
                n = heads.index((b, h))
                if n > 0:
                    e_lo.wait(e, heads[n - 1])
                if h == 0 and b > 0:
                    e_ll.wait(e, (2, b, 1))
                    e_r3.wait(e, (2, b - 1, NT - 2))
                e_nz.wait(e, (b, h, QORDER[-1]))
                for j in range(NT):
                    for i in range(j, NT):
                        src = P[h % 2][:, QBASE[i] + 128 * j:QBASE[i] + 128 * j + 128]
                        col = KBASE[j] + 128 * (i - j)
                        last = e.transpose(psB[:, col:col + 128], src, ident[:, :])
                e_tp.by(last, (b, h))

            def values(b, h):
                n = heads.index((b, h))
                if h == 0 and b > 0:
                    e_r3.wait(e, (2, b - 1, NT - 1))
                if n > 0:
                    e_oa.wait(e, heads[n - 1])
                e_lo.wait(e, (b, h))
                e_pl.wait(e, (b, ("v", h // 4, 1)))
                vv = v[(h // 4) % 2]
                for j in range(NT):
                    w = T - 128 * j
                    ks = slice(KBASE[j], KBASE[j] + w)
                    lhs = vv[:, j, h % 4, :]
                    mm(psC[:, 128 * j:T], lhs, pth[h % 2][:, ks], j == 0, False)
                    last = mm(psC[:, 128 * j:T], lhs, ptl[h % 2][:, ks], False, j == NT - 1)
                e_pv.by(last, (b, h))

            def attention(b):
                for s in range(H + 2):
                    if s < H:
                        scores(b, s)
                        for tile in tiles_of(s):
                            proj_tile(b, tile)
                        if s >= H - 2 and b + 1 < NB:
                            ln_transpose(1, b + 1, s - (H - 2))
                    if 1 <= s <= H:
                        transposes(b, s - 1)
                    if s >= 2:
                        values(b, s - 2)

            e_id.wait(e, "ident")
            for u in range(2):
                ln_transpose(1, 0, u)
            e_sl.wait(e, "wout")
            up(1, 0)
            for t in range(NT):
                dn(1, 0, t)
            for u in range(2):
                ln_transpose(2, 0, u)
            for tile in tiles_of(-1):
                proj_tile(0, tile)
            for b in B:
                more = b + 1 < NB
                attention(b)
                if more:
                    up(1, b + 1)
                for t in range(NT):
                    out_proj(b, t)
                if more:
                    dn(1, b + 1, 0)
                    dn(1, b + 1, 1)
                ln_transpose(3, b, 0)
                if more:
                    dn(1, b + 1, 2)
                ln_transpose(3, b, 1)
                if more:
                    dn(1, b + 1, 3)
                up(2, b)
                if more:
                    ln_transpose(2, b + 1, 0)
                dn(2, b, 0)
                if more:
                    ln_transpose(2, b + 1, 1)
                for t in range(1, NT):
                    dn(2, b, t)
                if more:
                    for tile in tiles_of(-1):
                        proj_tile(b + 1, tile)

        def tile_parts(tile, dst_lo):
            if tile[0] == "v":
                _, g, u = tile
                o64 = 64 if dst_lo else 0
                return (v[g % 2][:, 2 * u:2 * u + 2, :, o64:o64 + 64],
                        psD[:, :].rearrange("p (t h d) -> p t h d", t=2, h=4))
            plane = {"q": (0, 3), "k": (1, 2)}[tile[0]][1 if dst_lo else 0]
            return qk[:, plane, :], psD[:, :]

        def ln_source(L, u):
            return bk(7) if L == 1 else bk(3 + u)

        @block.scalar
        def _(e):
            def proj_hi(b, tile):
                e_pj.wait(e, (b, tile))
                if tile[0] in "qk":
                    c = tile[1]
                    if (b, c) != (0, 0):
                        pb, pc = (b, c - 1) if c else (b - 1, NC - 1)
                        if c or b:
                            e_sk[0].wait(e, (pb, 2 * pc, 2))
                            e_sk[1].wait(e, (pb, 2 * pc + 1, 2))
                elif tile[1] < 2 and b > 0:
                    e_pv.wait(e, (b - 1, H - 1))
                elif tile[1] >= 2:
                    e_pv.wait(e, (b, 4 * tile[1] - 5))
                dst, src = tile_parts(tile, False)
                e_ph.by(e.activation(dst, src, ACT.Copy), (b, tile))

            def ln_hi(L, b, u):
                e_lt.wait(e, (L, b, u))
                if L == 1 and b > 0:
                    e_pj.wait(e, (b - 1, tiles[-1]))
                if L == 2:
                    e_up.wait(e, (2, b - 1, NM - 1) if b > 0 else (1, 0, NM - 1))
                if L == 3 and b + 1 < NB:
                    e_up.wait(e, (1, b + 1, NM - 1))
                us = slice(256 * u, 256 * u + 256)
                e_lh.by(e.activation(xth[:, :, us], ln_source(L, u).rearrange("p (k n) -> p k n", k=2), ACT.Copy),
                        (L, b, u))

            def gelu(f, b):
                n0 = hidden.index((f, b, 0))
                for m in range(NM):
                    e_up.wait(e, (f, b, m))
                    if n0 + m >= 3:
                        e_gs.wait(e, hidden[n0 + m - 3])
                    e_gl.by(e.activation(gt[:, m % 3, :], bk(m % 3), ACT.Gelu, bias=b1c[:, m:m + 1]), (f, b, m))

            def out_hi(b, t):
                if t == 0:
                    e_oa.wait(e, (b, H - 1))
                if t >= 2:
                    e_ot.wait(e, (b, t - 2))
                e_oh.by(e.activation(oh[t % 2][:, :, :], o[:, :, 128 * t:128 * t + 128], ACT.Copy), (b, t))

            def exps(b, h):
                for i in QORDER:
                    e_tt.wait(e, (b, h, i))
                    p = P[h % 2][:, QBASE[i]:QBASE[i] + 128 * (i + 1)]
                    r = h % 4
                    e_ex.by(e.activation(p, p, ACT.Exp, bias=mx[:, r, i:i + 1], scale=-1.0,
                                         accum_out=sm[:, r, i:i + 1]), (b, h, i))

            def attention(b):
                for s in range(H + 3):
                    if s >= 3:
                        h = s - 3
                        e_pv.wait(e, (b, h))
                        e_oc.by(e.activation(o[64 * (h % 2):64 * (h % 2) + 64, h // 2, :], psC[64:128, :], ACT.Copy),
                                (b, h))
                    if s < H:
                        exps(b, s)
                        for tile in tiles_of(s):
                            proj_hi(b, tile)
                        if s >= H - 2 and b + 1 < NB:
                            ln_hi(1, b + 1, s - (H - 2))
                    if 1 <= s <= H:
                        h = s - 1
                        e_tp.wait(e, (b, h))
                        if h >= 2:
                            e_pv.wait(e, (b, h - 2))
                        e_hp.by(e.activation(pth[h % 2][:, :], psB[:, 0:PW], ACT.Copy), (b, h))

            def split_hi(key, dst, src, scale):
                e_sh.by(e.activation(dst, src, ACT.Copy, scale=scale), key)

            for u in range(2):
                ln_hi(1, 0, u)
            for n in ("w1", "w2"):
                e_w[n].wait(e, 0)
                split_hi(n, SH[n][0][:, :, :], SH[n][2][:, :, :], 0.5 if n == "w2" else 1.0)
            e_w["wqkv"].wait(e, 0)
            for h in range(H):
                split_hi(("q", h), wqh[:, :, qcols(h)], rawq[:, :, qcols(h)], q_scale(h))
            split_hi("kv", wqh[:, :, KV], rawq[:, :, KV], 1.0)
            e_w["wout"].wait(e, 0)
            split_hi("wout", woh[:, :, :], rawo[:, :, :], 1.0)
            e_w["b1"].wait(e, 0)
            e_sl.wait(e, "wout")
            gelu(1, 0)
            for u in range(2):
                ln_hi(2, 0, u)
            for tile in tiles_of(-1):
                proj_hi(0, tile)
            for b in B:
                more = b + 1 < NB
                attention(b)
                if more:
                    gelu(1, b + 1)
                for t in range(NT):
                    out_hi(b, t)
                for u in range(2):
                    ln_hi(3, b, u)
                gelu(2, b)
                if more:
                    for u in range(2):
                        ln_hi(2, b + 1, u)
                    for tile in tiles_of(-1):
                        proj_hi(b + 1, tile)

        @block.vector
        def _(e):
            xs = {1: x0, 2: x1, 3: x2}

            def residue(dst, src, hi):
                return e.tensor_tensor(dst, src, hi.bitcast(F32), ALU.subtract)

            def proj_lo(b, tile):
                e_ph.wait(e, (b, tile))
                dst, src = tile_parts(tile, True)
                hi, _ = tile_parts(tile, False)
                e_pl.by(residue(dst, src, hi), (b, tile))

            def ln_lo(L, b, u):
                e_lh.wait(e, (L, b, u))
                us = slice(256 * u, 256 * u + 256)
                e_ll.by(residue(xtl[:, :, us], ln_source(L, u).rearrange("p (k n) -> p k n", k=2), xth[:, :, us]),
                        (L, b, u))

            def stats(L, b, t):
                e_bs.by(e.bn_stats(st[:, L - 1, t, :], xs[L][:, t, :]), (L, b, t))
                e_bs.wait(e, (L, b, t))
                e_ba.by(e.bn_aggr(mv[:, L - 1, t, :], st[:, L - 1, t, :]), (L, b, t))

            def variance(L, b):
                e_ba.wait(e, (L, b, NT - 1))
                e_ve.by(e.tensor_scalar(ve[:, L - 1, :], mv[:, L - 1, :, 1], EPS, None, ALU.add), (L, b))

            def normal(L, b, t):
                if t == 0:
                    e_pw.wait(e, (L, b))
                    n = lns.index((L, b))
                    if n > 0:
                        e_lt.wait(e, (*lns[n - 1], 1))
                if t == 2:
                    e_lt.wait(e, (L, b, 0))
                e_xn.by(e.tensor_scalar(xn[:, t % 2, :], xs[L][:, t, :], mv[:, L - 1, t, 0:1], rstd[:, L - 1, t:t + 1],
                                        ALU.subtract, ALU.mult), (L, b, t))

            def add(events, key, produced, pkey, dst, other, L, b, t):
                produced.wait(e, pkey)
                e_pb.wait(e, (L, b))
                src = bk(5 + t % 2) if produced is e_dn else bk(3 + t % 2)
                events.by(e.tensor_tensor(dst[:, t, :], src[:, 0:D], other[:, t, :], ALU.add), key)
                events.wait(e, key)

            def add1(b, t):
                if t == 0 and b > 0:
                    e_r2.wait(e, (b - 1, NT - 1))
                add(e_r1, (1, b, t), e_dn, (1, b, t), x1, x0, 1, b, t)
                stats(2, b, t)

            def add2(b, t):
                if t == 0 and b > 0:
                    e_y.wait(e, b - 1)
                add(e_r2, (b, t), e_ot, (b, t), x2, x1, 2, b, t)
                stats(3, b, t)

            def add3(b, t):
                add(e_r3, (2, b, t), e_dn, (2, b, t), x2, x2, 3, b, t)

            def gelu_split(f, b):
                for m in range(NM):
                    e_gl.wait(e, (f, b, m))
                    e_gh.by(e.tensor_copy(gh[:, m, :], gt[:, m % 3, :]), (f, b, m))
                    e_gh.wait(e, (f, b, m))
                    e_gs.by(residue(gl[:, m, :], gt[:, m % 3, :], gh[:, m, :]), (f, b, m))

            def out_lo(b, t):
                e_oh.wait(e, (b, t))
                e_ol.by(residue(ol[t % 2][:, :, :], o[:, :, 128 * t:128 * t + 128], oh[t % 2][:, :, :]), (b, t))

            def attention(b):
                for s in range(H + 3):
                    if 2 <= s <= H + 1:
                        h = s - 2
                        e_hp.wait(e, (b, h))
                        e_lo.by(residue(ptl[h % 2][:, :], psB[:, 0:PW], pth[h % 2][:, :]), (b, h))
                    if s >= 3:
                        h = s - 3
                        e_oc.wait(e, (b, h))
                        dst = o[64 * (h % 2):64 * (h % 2) + 64, h // 2, :]
                        e_oa.by(e.tensor_tensor(dst, psC[0:64, :], dst, ALU.add), (b, h))
                    if s < H:
                        for n, i in enumerate(QORDER):
                            e_qk.wait(e, (b, s, 0 if i == 2 else i))
                            if n == 0 and s >= 2:
                                e_tp.wait(e, (b, s - 2))
                            w = 128 * (i + 1)
                            cs = slice(QBASE[i], QBASE[i] + w)
                            e_tt.by(e.tensor_tensor_reduce(
                                out=P[s % 2][:, cs], in0=psA[:, cs], in1=dist[:, T - w:T], scale=-SLOPE[s],
                                scalar=BIG, op0=ALU.add, op1=ALU.min, accum_out=mx[:, s % 4, i:i + 1]), (b, s, i))
                        for tile in tiles_of(s):
                            proj_lo(b, tile)
                        e_ex.wait(e, (b, s, QORDER[-1]))
                        e_rc.by(e.reciprocal(rs[:, s % 4, :], sm[:, s % 4, :]), (b, s))
                        if b + 1 < NB:
                            if s == 10:
                                e_x.wait(e, b + 1)
                                for t in range(NT):
                                    stats(1, b + 1, t)
                                variance(1, b + 1)
                            if s == 12:
                                normal(1, b + 1, 0)
                                normal(1, b + 1, 1)
                            if s == 14:
                                ln_lo(1, b + 1, 0)
                                normal(1, b + 1, 2)
                                normal(1, b + 1, 3)
                            if s == 15:
                                ln_lo(1, b + 1, 1)

            def split_lo(key, hi, lo, raw, scale):
                e_sh.wait(e, key)
                e_sl.by(e.scalar_tensor_tensor(lo, raw, scale, hi.bitcast(F32), ALU.mult, ALU.subtract), key)

            e_id.wait(e, "dist")
            e_x.wait(e, 0)
            for t in range(NT):
                stats(1, 0, t)
            variance(1, 0)
            for t in range(NT):
                normal(1, 0, t)
            for u in range(2):
                ln_lo(1, 0, u)
            for n in ("w1", "w2"):
                hi, lo, raw = SH[n]
                split_lo(n, hi[:, :, :], lo[:, :, :], raw[:, :, :], 0.5 if n == "w2" else 1.0)
            for h in range(H):
                split_lo(("q", h), wqh[:, :, qcols(h)], wql[:, :, qcols(h)], rawq[:, :, qcols(h)], q_scale(h))
            split_lo("kv", wqh[:, :, KV], wql[:, :, KV], rawq[:, :, KV], 1.0)
            split_lo("wout", woh[:, :, :], wol[:, :, :], rawo[:, :, :], 1.0)
            gelu_split(1, 0)
            for t in range(NT):
                add1(0, t)
            variance(2, 0)
            for t in range(NT):
                normal(2, 0, t)
            for u in range(2):
                ln_lo(2, 0, u)
            for tile in tiles_of(-1):
                proj_lo(0, tile)
            for b in B:
                more = b + 1 < NB
                attention(b)
                if more:
                    gelu_split(1, b + 1)
                out_lo(b, 0)
                out_lo(b, 1)
                add2(b, 0)
                out_lo(b, 2)
                add2(b, 1)
                out_lo(b, 3)
                add2(b, 2)
                add2(b, 3)
                variance(3, b)
                if more:
                    add1(b + 1, 0)
                normal(3, b, 0)
                normal(3, b, 1)
                if more:
                    add1(b + 1, 1)
                ln_lo(3, b, 0)
                normal(3, b, 2)
                normal(3, b, 3)
                if more:
                    add1(b + 1, 2)
                ln_lo(3, b, 1)
                if more:
                    add1(b + 1, 3)
                    variance(2, b + 1)
                gelu_split(2, b)
                if more:
                    normal(2, b + 1, 0)
                    normal(2, b + 1, 1)
                    ln_lo(2, b + 1, 0)
                    normal(2, b + 1, 2)
                    normal(2, b + 1, 3)
                add3(b, 0)
                if more:
                    ln_lo(2, b + 1, 1)
                for t in range(1, NT):
                    add3(b, t)
                if more:
                    for tile in tiles_of(-1):
                        proj_lo(b + 1, tile)

        @block.gpsimd
        def _(e):
            def power(L, b):
                e_ve.wait(e, (L, b))
                e_pw.by(e.tensor_tensor(rstd[:, L - 1, :], ve[:, L - 1, :], mhalf[:, :], ALU.pow), (L, b))

            def bias(L, b):
                e_xn.wait(e, (L, b, NT - 1))
                xs, bb = {1: (x0, b2h), 2: (x1, bo), 3: (x2, b2h)}[L]
                bb = bb[:, :].unsqueeze(1).broadcast_to([128, NT, D])
                e_pb.by(e.tensor_tensor(xs[:, :, :], xs[:, :, :], bb, ALU.add), (L, b))

            def attention(b):
                for s in range(H):
                    e_rc.wait(e, (b, s))
                    for i in QORDER:
                        p = P[s % 2][:, QBASE[i]:QBASE[i] + 128 * (i + 1)]
                        e_nz.by(e.tensor_scalar(p, p, rs[:, s % 4, i:i + 1], 1.0, ALU.mult, ALU.mult), (b, s, i))
                    if b + 1 < NB:
                        if s == 10:
                            power(1, b + 1)
                        if s == 15:
                            bias(1, b + 1)

            e_id.by(e.memset(ident[:, :], 0.0), "zero")
            e_id.wait(e, "zero")
            e_id.by(e.affine_select(out=ident[:, :], in_=ident[:, :], compare_op=ALU.not_equal, fill=1.0,
                                    base=0, pattern=[[-1, 128]], channel_multiplier=1), "ident")
            e_id.by(e.iota(dist[:, :], [[1, T]], base=-(T - 128), channel_multiplier=-1,
                           allow_small_or_imprecise_dtypes=True), "iota")
            e_id.wait(e, "iota")
            e_id.by(e.affine_select(out=dist[:, :], in_=dist[:, :], compare_op=ALU.is_ge, fill=-BIG,
                                    base=T - 128, pattern=[[-1, T]], channel_multiplier=1), "dist")
            e_id.by(e.memset(mhalf[:, :], -0.5), "mhalf")
            e_id.wait(e, "mhalf")
            power(1, 0)
            e_w["b2"].wait(e, 0)
            e_sb.by(e.tensor_scalar(b2h[:, :], b2h[:, :], 0.5, 1.0, ALU.mult, ALU.mult), "w2")
            e_sb.wait(e, "w2")
            bias(1, 0)
            power(2, 0)
            e_w["bout"].wait(e, 0)
            bias(2, 0)
            for b in B:
                attention(b)
                power(3, b)
                bias(3, b)
                if b + 1 < NB:
                    power(2, b + 1)
                    bias(2, b + 1)


INPUTS = ["L0_attn_x", "L0_attn_w_qkv", "L0_attn_w_out", "L0_attn_b_out",
          "L0_ffn_w1", "L0_ffn_b1", "L0_ffn_w2", "L0_ffn_b2"]


def kernel(**inputs):
    import numpy as np
    import concourse.bacc as bacc
    from concourse import mybir
    from concourse.bass_utils import run_bass_kernel_spmd

    nc = bacc.Bacc("TRN2", target_bir_lowering=False, num_devices=1)
    arrays, args = {}, []
    for name in INPUTS:
        a = np.ascontiguousarray(inputs[name])
        arrays["in_" + name] = a
        args.append(nc.dram_tensor("in_" + name, a.shape, mybir.dt.from_np(a.dtype), kind="ExternalInput").ap())
    y = nc.dram_tensor("out_y", inputs["L0_attn_x"].shape, mybir.dt.float32, kind="ExternalOutput").ap()
    build(nc, *args, y)
    r = run_bass_kernel_spmd(nc, [arrays], core_ids=[0])
    return r.results[0]["out_y"]
```

```python
def build(nc, x_d, w_qkv_d, w_out_d, b_out_d, w1_d, b1_d, w2_d, b2_d, y_d):
    from concourse import mybir

    F32 = mybir.dt.float32
    F32R = mybir.dt.float32r
    I32 = mybir.dt.int32
    ALU = mybir.AluOpType
    ACT = mybir.ActivationFunctionType

    NB = x_d.shape[0]
    T, D, H, DH, F = 512, 256, 16, 64, 1024
    NT, NK, NM, NC = T // 128, D // 128, F // 128, H // 2
    EPS = 1e-5
    BIG = 3.0e38
    SLOPE = [2.0 ** (-0.5 * (h + 1)) for h in range(H)]
    BASE = {3: 0, 2: 512, 0: 896, 1: 1024}
    QBASE = BASE
    KBASE = {0: 0, 1: 512, 3: 896, 2: 1024}
    QORDER = (3, 2, 0, 1)
    PW = 1280

    at = [16512]

    def place(name, shape, dt, offset=None):
        n = 4
        for s in shape[1:]:
            n *= s
        if offset is None:
            offset = at[0]
            at[0] += -(-n // 32) * 32
        assert offset + n <= nc.sbuf_usable_end, name
        return nc.alloc_sbuf_tensor_at(name, list(shape), dt, offset=offset)

    w1h, w1l = place("w1h", [128, NK, F], F32R), place("w1l", [128, NK, F], F32R)
    w2h, w2l = place("w2h", [128, NM, D], F32R), place("w2l", [128, NM, D], F32R)
    wqh, wql = place("wqh", [128, NK, 3 * H * DH], F32R), place("wql", [128, NK, 3 * H * DH], F32R)
    woh, wol = place("woh", [128, NC, D], F32R), place("wol", [128, NC, D], F32R)
    dist = place("dist", [128, T], F32)
    ident = place("ident", [128, 128], F32)
    b2h = place("b2h", [128, D], F32)
    bo = place("bo", [128, D], F32)
    b1c = place("b1c", [128, NM], F32)
    mhalf = place("mhalf", [128, NT], F32)
    st = place("st", [128, 3, NT, 6], F32)
    mv = place("mv", [128, 3, NT, 2], F32)
    ve = place("ve", [128, 3, NT], F32)
    rstd = place("rstd", [128, 3, NT], F32)
    mx = place("mx", [128, 4, NT], F32)
    sm = place("sm", [128, 4, NT], F32)
    rs = place("rs", [128, 4, NT], F32)
    x0 = place("x0", [128, NT, D], F32)
    x1 = place("x1", [128, NT, D], F32)
    x2 = place("x2", [128, NT, D], F32)
    xn = place("xn", [128, 2, D], F32)
    xth, xtl = place("xth", [128, NK, T], F32R), place("xtl", [128, NK, T], F32R)
    o = place("o", [128, NC, T], F32)

    R = at[0]
    qk = place("qk", [128, 4, T], F32R, R)
    stack = [place(f"stack{i}", [128, 3, T], F32R, R + 8192 + 6144 * i) for i in range(2)]
    v = [place(f"v{i}", [128, NT, 4, 128], F32R, R + 20480 + 8192 * i) for i in range(2)]
    P = [place(f"P{i}", [128, PW], F32, R + 36864 + 4 * PW * i) for i in range(2)]
    pth = [place(f"pth{i}", [128, PW], F32R, R + 47104 + 8 * PW * i) for i in range(2)]
    ptl = [place(f"ptl{i}", [128, PW], F32R, R + 47104 + 4 * PW + 8 * PW * i) for i in range(2)]
    gh = place("gh", [128, NM, T], F32R, R + 34816)
    gl = place("gl", [128, NM, T], F32R, R + 34816 + 16384)
    oh = [place(f"oh{i}", [128, NC, 128], F32R, R + 8192 * i) for i in range(2)]
    ol = [place(f"ol{i}", [128, NC, 128], F32R, R + 4096 + 8192 * i) for i in range(2)]
    gt = place("gt", [128, 3, T], F32, R + 16384)
    raw1 = place("raw1", [128, NK, F], F32, R)
    raw2 = place("raw2", [128, NM, D], F32, R + 8192)
    rawo = place("rawo", [128, NC, D], F32, R + 16384)
    rawq = place("rawq", [128, NK, 3 * H * DH], F32, R + 24576)
    iota = place("iota", [128, T], I32, R + 49152)

    psA = nc.alloc_psum_tensor("psA", [128, 3 * 512], F32)
    psB = nc.alloc_psum_tensor("psB", [128, 3 * 512], F32)
    psC = nc.alloc_psum_tensor("psC", [128, 512], F32)
    psD = nc.alloc_psum_tensor("psD", [128, 512], F32)

    def bk(i):
        if i < 3:
            return psA[:, 512 * i:512 * i + 512]
        if i < 6:
            return psB[:, 512 * (i - 3):512 * (i - 3) + 512]
        return (psC if i == 6 else psD)[:, :]

    PE_STEP = [("scores", 0), ("first", 0), ("norm", 0), ("transposes", 1), ("second", 0), ("values", 2)]
    ACT_STEP = [("exp a", 0), ("first", 0), ("norm", 0), ("exp b", 0), ("hi", 1), ("second", 0), ("half", 2)]
    DVE_STEP = [("max", 0), ("add", 3), ("1/sum a", 0), ("first", 0), ("1/sum b", 0), ("norm", 0), ("lo", 1),
                ("second", 0)]

    B = range(NB)
    ffn = [(1, 0)] + [e for b in B for e in ([(1, b + 1)] if b + 1 < NB else []) + [(2, b)]]
    lns = [(1, 0), (2, 0)] + [e for b in B for e in (
        [(1, b + 1), (3, b), (2, b + 1)] if b + 1 < NB else [(3, b)])]

    def tiles_of(s):
        if s == -1:
            return [("q", 0), ("k", 0), ("v", 0, 0)]
        c, odd = divmod(s, 2)
        if odd:
            g, u = divmod(c + 1, 2)
            return [("v", g, u)] if g < 4 else []
        return [("q", c + 1), ("k", c + 1)] if c + 1 < NC else []

    def slots(s):
        t = tiles_of(s) if s < H else []
        return t[:1], t[1:]

    tiles = [t for s in range(-1, H) for t in tiles_of(s)]
    heads = [(b, h) for b in B for h in range(H)]
    per_block = [(b, h, i) for b, h in heads for i in QORDER]
    units = [(L, b, u) for L, b in lns for u in range(2)]
    rows = [(L, b, t) for L, b in lns for t in range(NT)]
    hidden = [(f, b, m) for f, b in ffn for m in range(NM)]
    down = [(f, b, t) for f, b in ffn for t in range(NT)]
    outs = [(b, t) for b in B for t in range(NT)]
    proj = [(b, t) for b in B for t in tiles]

    class Events:
        def __init__(self, name, keys, step=1):
            self.sem, self.step, self.made = nc.alloc_semaphore(name), step, 0
            self.keys = list(keys)
            self.value = {k: step * (n + 1) for n, k in enumerate(self.keys)}

        def by(self, instruction, key):
            assert self.keys[self.made] == key, (self.sem, key, self.keys[self.made])
            self.made += 1
            instruction.then_inc(self.sem, self.step)

        def wait(self, engine, key):
            engine.wait_ge(self.sem, self.value[key])

    e_qk = Events("qk_done", per_block)
    e_tp = Events("tp_done", heads)
    e_pv = Events("pv_done", heads)
    e_pj = Events("pj_done", proj)
    e_lt = Events("lt_done", units)
    e_up = Events("up_done", hidden)
    e_dn = Events("dn_done", down)
    e_ot = Events("ot_done", outs)
    e_ex = Events("ex_done", per_block)
    e_hp = Events("hp_done", heads)
    e_oc = Events("oc_done", heads)
    e_ph = Events("ph_done", proj)
    e_lh = Events("lh_done", units)
    e_gl = Events("gl_done", hidden)
    e_oh = Events("oh_done", outs)
    e_tt = Events("tt_done", per_block)
    e_rc = Events("rc_done", [(b, h, half) for b, h in heads for half in (1, 0)])
    e_lo = Events("lo_done", heads)
    e_oa = Events("oa_done", heads)
    e_pl = Events("pl_done", proj)
    e_ll = Events("ll_done", units)
    e_gh = Events("gh_done", hidden)
    e_gs = Events("gs_done", hidden)
    e_ol = Events("ol_done", outs)
    e_r1 = Events("r1_done", [(f, b, t) for f, b, t in down if f == 1])
    e_r3 = Events("r3_done", [(f, b, t) for f, b, t in down if f == 2])
    e_r2 = Events("r2_done", outs)
    e_bs = Events("bs_done", rows)
    e_ba = Events("ba_done", rows)
    e_ve = Events("ve_done", lns)
    e_xn = Events("xn_done", rows)
    e_nz = Events("nz_done", per_block)
    e_pw = Events("pw_done", lns)
    e_pb = Events("pb_done", lns)
    e_x = Events("x_in", list(B), 16)
    e_y = Events("y_out", list(B), 16)
    e_sq = [Events(f"stack_q{i}", [(b, h, n) for b, h in heads if h % 2 == i for n in range(2)], 16)
            for i in range(2)]
    e_sk = [Events(f"stack_k{i}", [(b, h, n) for b, h in heads if h % 2 == i for n in range(2)], 16)
            for i in range(2)]
    names = ["w1", "b1", "w2", "b2", "wqkv", "wout", "bout"]
    e_w = {n: Events("in_" + n, [0], 16) for n in names}
    e_sh = Events("set_hi", ["w1", "w2"] + [("q", h) for h in range(H)] + ["kv", "wout"])
    e_sl = Events("set_lo", ["w1", "w2"] + [("q", h) for h in range(H)] + ["kv", "wout"])
    e_sb = Events("set_bias", ["b2"])
    e_id = Events("set_ident", ["zero", "ident", "iota", "dist", "mhalf"])

    SH = {"w1": (w1h, w1l, raw1), "w2": (w2h, w2l, raw2), "wout": (woh, wol, rawo)}

    def qcols(h):
        return slice(h * DH, (h + 1) * DH)

    HD = H * DH
    KV = slice(HD, 3 * HD)

    def q_scale(h):
        return DH ** -0.5 / SLOPE[h]

    block = nc.Block()
    with block:
        @block.sync
        def _(e):
            e_w_in = [
                ("w1", raw1[:, :, :], w1_d.rearrange("(k p) n -> p k n", p=128)),
                ("b1", b1c[:, :], b1_d.rearrange("(m p) -> p m", p=128)),
                ("w2", raw2[:, :, :], w2_d.rearrange("(m p) n -> p m n", p=128)),
                ("b2", b2h[:, :], b2_d.partition_broadcast(128)),
                ("wqkv", rawq[:, :, :], w_qkv_d.rearrange("(k p) n -> p k n", p=128)),
                ("wout", rawo[:, :, :], w_out_d.rearrange("(c p) n -> p c n", p=128)),
                ("bout", bo[:, :], b_out_d.partition_broadcast(128)),
            ]

            def load_x(b):
                if b > 0:
                    e_r1.wait(e, (1, b - 1, NT - 1))
                e_x.by(e.dma_start(x0[:, :, :], x_d[b].rearrange("(t p) n -> p t n", p=128)), b)

            load_x(0)
            for n, dst, src in e_w_in:
                e_w[n].by(e.dma_start(dst, src, allow_slow_non_contiguous=(n == "b1")), 0)

            def stack_head(b, h):
                c, i = h // 2, h % 2
                src = qk[64 * i:64 * i + 64, :, :].bitcast(F32)
                dst = stack[i]
                e_pl.wait(e, (b, ("q", c)))
                n = heads.index((b, h))
                if n >= 2:
                    e_qk.wait(e, (*heads[n - 2], QORDER[-1]))
                e_sq[i].by(e.dma_start(dst[0:64, 0, :].bitcast(F32), src[:, 0, :]), (b, h, 0))
                e_sq[i].by(e.dma_start(dst[64:128, 0, :].bitcast(F32), src[:, 3, :]), (b, h, 1))
                e_pl.wait(e, (b, ("k", c)))
                for half in range(2):
                    e_sk[i].by(e.dma_start(dst[64 * half:64 * half + 64, 1:3, :].bitcast(F32), src[:, 1:3, :]),
                               (b, h, half))

            for b in B:
                stack_head(b, 0)
                stack_head(b, 1)
                if b + 1 < NB:
                    load_x(b + 1)
                for h in range(2, H):
                    stack_head(b, h)
                e_r3.wait(e, (2, b, NT - 1))
                e_y.by(e.dma_start(y_d[b].rearrange("(t p) n -> p t n", p=128), x2[:, :, :]), b)
            e_y.wait(e, NB - 1)

        @block.tensor
        def _(e):
            def mm(out, lhsT, rhs, first, last):
                return e.matmul(out, lhsT, rhs, start=first, stop=last)

            def three(out, pairs):
                n = len(pairs)
                for i, (ah, al, bh, bl) in enumerate(pairs):
                    mm(out, ah, bh, i == 0, False)
                    mm(out, ah, bl, False, False)
                    inst = mm(out, al, bh, False, i == n - 1)
                return inst

            def ln_transpose(L, b, u):
                dst = bk(7) if L == 1 else bk(3 + u)
                n = units.index((L, b, u))
                if L == 1:
                    if u == 1:
                        e_ll.wait(e, (L, b, 0))
                    elif b > 0:
                        e_pl.wait(e, (b - 1, tiles[-1]))
                elif L == 3:
                    e_r2.wait(e, (b, 2 + u))
                elif b > 0:
                    e_ll.wait(e, (3, b - 1, u))
                for t in (2 * u, 2 * u + 1):
                    e_xn.wait(e, (L, b, t))
                    for k in range(NK):
                        col = k * 256 + (t - 2 * u) * 128
                        last = e.transpose(dst[:, col:col + 128], xn[:, t % 2, k * 128:(k + 1) * 128], ident[:, :])
                e_lt.by(last, (L, b, u))

            def up(f, b):
                L = 1 if f == 1 else 3
                e_ll.wait(e, (L, b, 1))
                if f == 1 and b > 0:
                    e_tt.wait(e, (b - 1, H - 1, QORDER[-1]))
                if f == 2 and b + 1 < NB:
                    e_gl.wait(e, (1, b + 1, NM - 1))
                if f == 2 and b + 1 == NB:
                    e_tt.wait(e, (b, H - 1, QORDER[-1]))
                for m in range(NM):
                    if m >= 3:
                        e_gl.wait(e, (f, b, m - 3))
                    ms = slice(m * 128, m * 128 + 128)
                    last = three(bk(m % 3), [(w1h[:, k, ms], w1l[:, k, ms], xth[:, k, :], xtl[:, k, :])
                                             for k in range(NK)])
                    e_up.by(last, (f, b, m))

            def dn(f, b, t):
                if t >= 2:
                    (e_r1 if f == 1 else e_r3).wait(e, (f, b, t - 2))
                elif f == 1 and b > 0:
                    e_lo.wait(e, (b - 1, H - 1))
                    e_oa.wait(e, (b - 1, H - 1))
                elif f == 2 and b + 1 < NB:
                    e_r1.wait(e, (1, b + 1, NT - 2 + t))
                elif f == 2:
                    e_lo.wait(e, (b, H - 1))
                    e_oa.wait(e, (b, H - 1))
                e_gs.wait(e, (f, b, NM - 1))
                ts = slice(t * 128, t * 128 + 128)
                last = three(bk(5 + t % 2)[:, 0:D], [(gh[:, m, ts], gl[:, m, ts], w2h[:, m, :], w2l[:, m, :])
                                                   for m in range(NM)])
                e_dn.by(last, (f, b, t))

            def out_proj(b, t):
                if t >= 2:
                    e_r2.wait(e, (b, t - 2))
                else:
                    e_lo.wait(e, (b, H - 1))
                e_ol.wait(e, (b, t))
                i = t % 2
                last = three(bk(3 + i)[:, 0:D], [(oh[i][:, c, :], ol[i][:, c, :], woh[:, c, :], wol[:, c, :])
                                               for c in range(NC)])
                e_ot.by(last, (b, t))

            def proj_tile(b, tile):
                n = proj.index((b, tile))
                if tile == tiles[0]:
                    e_ll.wait(e, (2, b, 1))
                    if b > 0:
                        e_ll.wait(e, (1, b, 1))
                if n > 0:
                    e_pl.wait(e, proj[n - 1])
                dst = bk(7)
                if tile[0] == "v":
                    _, g, u = tile
                    gs = slice(2 * HD + g * 256, 2 * HD + g * 256 + 256)
                    for j in range(2):
                        ts = slice((2 * u + j) * 128, (2 * u + j) * 128 + 128)
                        last = three(dst[:, j * 256:j * 256 + 256],
                                     [(xth[:, k, ts], xtl[:, k, ts], wqh[:, k, gs], wql[:, k, gs])
                                      for k in range(NK)])
                else:
                    kind, c = tile
                    cs = slice((HD if kind == "k" else 0) + c * 128, (HD if kind == "k" else 0) + c * 128 + 128)
                    last = three(dst, [(wqh[:, k, cs], wql[:, k, cs], xth[:, k, :], xtl[:, k, :])
                                       for k in range(NK)])
                e_pj.by(last, (b, tile))

            def scores(b, h):
                n = heads.index((b, h))
                sk = stack[h % 2]
                e_sq[h % 2].wait(e, (b, h, 1))
                e_sk[h % 2].wait(e, (b, h, 1))
                if h == 0 and b > 0:
                    e_gl.wait(e, (2, b - 1, NM - 1))
                for i in QORDER:
                    if n > 0:
                        e_tt.wait(e, (*heads[n - 1], 0 if i == 2 else i))
                    w = 128 * (i + 1)
                    dst = psA[:, QBASE[i]:QBASE[i] + w]
                    qs = sk[:, 0, i * 128:i * 128 + 128]
                    mm(dst, qs, sk[:, 1, 0:w], True, False)
                    e_qk.by(mm(dst, qs, sk[:, 2, 0:w], False, True), (b, h, i))

            def transposes(b, h):
                n = heads.index((b, h))
                if n > 0:
                    e_lo.wait(e, heads[n - 1])
                if h == 0 and b > 0:
                    e_ll.wait(e, (2, b, 1))
                    e_r3.wait(e, (2, b - 1, NT - 2))
                e_nz.wait(e, (b, h, QORDER[-1]))
                for j in range(NT):
                    for i in range(j, NT):
                        src = P[h % 2][:, QBASE[i] + 128 * j:QBASE[i] + 128 * j + 128]
                        col = KBASE[j] + 128 * (i - j)
                        last = e.transpose(psB[:, col:col + 128], src, ident[:, :])
                e_tp.by(last, (b, h))

            def values(b, h):
                n = heads.index((b, h))
                if h == 0 and b > 0:
                    e_r3.wait(e, (2, b - 1, NT - 1))
                if n > 0:
                    e_oa.wait(e, heads[n - 1])
                e_lo.wait(e, (b, h))
                e_pl.wait(e, (b, ("v", h // 4, 1)))
                vv = v[(h // 4) % 2]
                for j in range(NT):
                    w = T - 128 * j
                    ks = slice(KBASE[j], KBASE[j] + w)
                    lhs = vv[:, j, h % 4, :]
                    mm(psC[:, 128 * j:T], lhs, pth[h % 2][:, ks], j == 0, False)
                    last = mm(psC[:, 128 * j:T], lhs, ptl[h % 2][:, ks], False, j == NT - 1)
                e_pv.by(last, (b, h))

            def attention(b):
                for s in range(H + 3):
                    first, second = slots(s)
                    for what, lag in PE_STEP:
                        h = s - lag
                        if what == "first":
                            for tile in first:
                                proj_tile(b, tile)
                        elif what == "second":
                            for tile in second:
                                proj_tile(b, tile)
                        elif what == "norm":
                            if H - 2 <= s < H and b + 1 < NB:
                                ln_transpose(1, b + 1, s - (H - 2))
                        elif 0 <= h < H:
                            {"scores": scores, "transposes": transposes, "values": values}[what](b, h)

            e_id.wait(e, "ident")
            for u in range(2):
                ln_transpose(1, 0, u)
            e_sl.wait(e, "wout")
            up(1, 0)
            for t in range(NT):
                dn(1, 0, t)
            for u in range(2):
                ln_transpose(2, 0, u)
            for tile in tiles_of(-1):
                proj_tile(0, tile)
            for b in B:
                more = b + 1 < NB
                attention(b)
                if more:
                    up(1, b + 1)
                for t in range(NT):
                    out_proj(b, t)
                if more:
                    dn(1, b + 1, 0)
                    dn(1, b + 1, 1)
                ln_transpose(3, b, 0)
                if more:
                    dn(1, b + 1, 2)
                ln_transpose(3, b, 1)
                if more:
                    dn(1, b + 1, 3)
                up(2, b)
                if more:
                    ln_transpose(2, b + 1, 0)
                dn(2, b, 0)
                if more:
                    ln_transpose(2, b + 1, 1)
                for t in range(1, NT):
                    dn(2, b, t)
                if more:
                    for tile in tiles_of(-1):
                        proj_tile(b + 1, tile)

        def tile_parts(tile, dst_lo):
            if tile[0] == "v":
                _, g, u = tile
                o64 = 64 if dst_lo else 0
                return (v[g % 2][:, 2 * u:2 * u + 2, :, o64:o64 + 64],
                        psD[:, :].rearrange("p (t h d) -> p t h d", t=2, h=4))
            plane = {"q": (0, 3), "k": (1, 2)}[tile[0]][1 if dst_lo else 0]
            return qk[:, plane, :], psD[:, :]

        def ln_source(L, u):
            return bk(7) if L == 1 else bk(3 + u)

        @block.scalar
        def _(e):
            def proj_hi(b, tile):
                e_pj.wait(e, (b, tile))
                if tile[0] in "qk":
                    c = tile[1]
                    if (b, c) != (0, 0):
                        pb, pc = (b, c - 1) if c else (b - 1, NC - 1)
                        for i, stacked in enumerate(e_sq if tile[0] == "q" else e_sk):
                            stacked.wait(e, (pb, 2 * pc + i, 1))
                elif tile[1] < 2:
                    if b > 0:
                        e_pv.wait(e, (b - 1, H - 1))
                else:
                    e_pv.wait(e, (b, 4 * tile[1] - 5))
                dst, src = tile_parts(tile, False)
                e_ph.by(e.activation(dst, src, ACT.Copy), (b, tile))

            def ln_hi(L, b, u):
                e_lt.wait(e, (L, b, u))
                if L == 1 and b > 0:
                    e_pj.wait(e, (b - 1, tiles[-1]))
                if L == 2:
                    e_up.wait(e, (2, b - 1, NM - 1) if b > 0 else (1, 0, NM - 1))
                if L == 3 and b + 1 < NB:
                    e_up.wait(e, (1, b + 1, NM - 1))
                us = slice(256 * u, 256 * u + 256)
                e_lh.by(e.activation(xth[:, :, us], ln_source(L, u).rearrange("p (k n) -> p k n", k=2), ACT.Copy),
                        (L, b, u))

            def gelu(f, b):
                n0 = hidden.index((f, b, 0))
                for m in range(NM):
                    e_up.wait(e, (f, b, m))
                    if n0 + m >= 3:
                        e_gs.wait(e, hidden[n0 + m - 3])
                    e_gl.by(e.activation(gt[:, m % 3, :], bk(m % 3), ACT.Gelu, bias=b1c[:, m:m + 1]), (f, b, m))

            def out_hi(b, t):
                if t == 0:
                    e_oa.wait(e, (b, H - 1))
                if t >= 2:
                    e_ot.wait(e, (b, t - 2))
                e_oh.by(e.activation(oh[t % 2][:, :, :], o[:, :, 128 * t:128 * t + 128], ACT.Copy), (b, t))

            def exps(b, h, blocks):
                for i in blocks:
                    e_tt.wait(e, (b, h, i))
                    p = P[h % 2][:, QBASE[i]:QBASE[i] + 128 * (i + 1)]
                    r = h % 4
                    e_ex.by(e.activation(p, p, ACT.Exp, bias=mx[:, r, i:i + 1], scale=-1.0,
                                         accum_out=sm[:, r, i:i + 1]), (b, h, i))

            def attention(b):
                for s in range(H + 3):
                    first, second = slots(s)
                    for what, lag in ACT_STEP:
                        h = s - lag
                        if what == "first":
                            for tile in first:
                                proj_hi(b, tile)
                        elif what == "second":
                            for tile in second:
                                proj_hi(b, tile)
                        elif what == "norm":
                            if H - 2 <= s < H and b + 1 < NB:
                                ln_hi(1, b + 1, s - (H - 2))
                        elif not 0 <= h < H:
                            pass
                        elif what == "exp a":
                            exps(b, h, QORDER[:2])
                        elif what == "exp b":
                            exps(b, h, QORDER[2:])
                        elif what == "hi":
                            e_tp.wait(e, (b, h))
                            if h >= 2:
                                e_pv.wait(e, (b, h - 2))
                            e_hp.by(e.activation(pth[h % 2][:, :], psB[:, 0:PW], ACT.Copy), (b, h))
                        elif what == "half":
                            e_pv.wait(e, (b, h))
                            e_oc.by(e.activation(o[64 * (h % 2):64 * (h % 2) + 64, h // 2, :], psC[64:128, :],
                                                 ACT.Copy), (b, h))

            def split_hi(key, dst, src, scale):
                e_sh.by(e.activation(dst, src, ACT.Copy, scale=scale), key)

            for u in range(2):
                ln_hi(1, 0, u)
            for n in ("w1", "w2"):
                e_w[n].wait(e, 0)
                split_hi(n, SH[n][0][:, :, :], SH[n][2][:, :, :], 0.5 if n == "w2" else 1.0)
            e_w["wqkv"].wait(e, 0)
            for h in range(H):
                split_hi(("q", h), wqh[:, :, qcols(h)], rawq[:, :, qcols(h)], q_scale(h))
            split_hi("kv", wqh[:, :, KV], rawq[:, :, KV], 1.0)
            e_w["wout"].wait(e, 0)
            split_hi("wout", woh[:, :, :], rawo[:, :, :], 1.0)
            e_w["b1"].wait(e, 0)
            e_sl.wait(e, "wout")
            gelu(1, 0)
            for u in range(2):
                ln_hi(2, 0, u)
            for tile in tiles_of(-1):
                proj_hi(0, tile)
            for b in B:
                more = b + 1 < NB
                attention(b)
                if more:
                    gelu(1, b + 1)
                for t in range(NT):
                    out_hi(b, t)
                for u in range(2):
                    ln_hi(3, b, u)
                gelu(2, b)
                if more:
                    for u in range(2):
                        ln_hi(2, b + 1, u)
                    for tile in tiles_of(-1):
                        proj_hi(b + 1, tile)

        @block.vector
        def _(e):
            xs = {1: x0, 2: x1, 3: x2}

            def residue(dst, src, hi):
                return e.tensor_tensor(dst, src, hi.bitcast(F32), ALU.subtract)

            def proj_lo(b, tile):
                e_ph.wait(e, (b, tile))
                dst, src = tile_parts(tile, True)
                hi, _ = tile_parts(tile, False)
                e_pl.by(residue(dst, src, hi), (b, tile))

            def ln_lo(L, b, u):
                e_lh.wait(e, (L, b, u))
                us = slice(256 * u, 256 * u + 256)
                e_ll.by(residue(xtl[:, :, us], ln_source(L, u).rearrange("p (k n) -> p k n", k=2), xth[:, :, us]),
                        (L, b, u))

            def stats(L, b, t):
                e_bs.by(e.bn_stats(st[:, L - 1, t, :], xs[L][:, t, :]), (L, b, t))
                e_bs.wait(e, (L, b, t))
                e_ba.by(e.bn_aggr(mv[:, L - 1, t, :], st[:, L - 1, t, :]), (L, b, t))

            def variance(L, b):
                e_ba.wait(e, (L, b, NT - 1))
                e_ve.by(e.tensor_scalar(ve[:, L - 1, :], mv[:, L - 1, :, 1], EPS, None, ALU.add), (L, b))

            def normal(L, b, t):
                if t == 0:
                    e_pw.wait(e, (L, b))
                    n = lns.index((L, b))
                    if n > 0:
                        e_lt.wait(e, (*lns[n - 1], 1))
                if t == 2:
                    e_lt.wait(e, (L, b, 0))
                e_xn.by(e.tensor_scalar(xn[:, t % 2, :], xs[L][:, t, :], mv[:, L - 1, t, 0:1], rstd[:, L - 1, t:t + 1],
                                        ALU.subtract, ALU.mult), (L, b, t))

            def add(events, key, produced, pkey, dst, other, L, b, t):
                produced.wait(e, pkey)
                e_pb.wait(e, (L, b))
                src = bk(5 + t % 2) if produced is e_dn else bk(3 + t % 2)
                events.by(e.tensor_tensor(dst[:, t, :], src[:, 0:D], other[:, t, :], ALU.add), key)
                events.wait(e, key)

            def add1(b, t):
                if t == 0 and b > 0:
                    e_r2.wait(e, (b - 1, NT - 1))
                add(e_r1, (1, b, t), e_dn, (1, b, t), x1, x0, 1, b, t)
                stats(2, b, t)

            def add2(b, t):
                if t == 0 and b > 0:
                    e_y.wait(e, b - 1)
                add(e_r2, (b, t), e_ot, (b, t), x2, x1, 2, b, t)
                stats(3, b, t)

            def add3(b, t):
                add(e_r3, (2, b, t), e_dn, (2, b, t), x2, x2, 3, b, t)

            def gelu_split(f, b):
                for m in range(NM):
                    e_gl.wait(e, (f, b, m))
                    e_gh.by(e.tensor_copy(gh[:, m, :], gt[:, m % 3, :]), (f, b, m))
                    e_gh.wait(e, (f, b, m))
                    e_gs.by(residue(gl[:, m, :], gt[:, m % 3, :], gh[:, m, :]), (f, b, m))

            def out_lo(b, t):
                e_oh.wait(e, (b, t))
                e_ol.by(residue(ol[t % 2][:, :, :], o[:, :, 128 * t:128 * t + 128], oh[t % 2][:, :, :]), (b, t))

            def inverse(b, h, half):
                e_ex.wait(e, (b, h, 2 if half else 1))
                cs = slice(2 * half, 2 * half + 2)
                e_rc.by(e.reciprocal(rs[:, h % 4, cs], sm[:, h % 4, cs]), (b, h, half))

            def biased(b, h):
                for n, i in enumerate(QORDER):
                    e_qk.wait(e, (b, h, 0 if i == 2 else i))
                    if n == 0 and h >= 2:
                        e_tp.wait(e, (b, h - 2))
                    w = 128 * (i + 1)
                    cs = slice(QBASE[i], QBASE[i] + w)
                    e_tt.by(e.tensor_tensor_reduce(
                        out=P[h % 2][:, cs], in0=psA[:, cs], in1=dist[:, T - w:T], scale=-SLOPE[h],
                        scalar=BIG, op0=ALU.add, op1=ALU.min, accum_out=mx[:, h % 4, i:i + 1]), (b, h, i))

            def norm_step(b, s):
                if s == 9:
                    e_x.wait(e, b + 1)
                if 9 <= s < 9 + NT:
                    stats(1, b + 1, s - 9)
                if s == 9 + NT - 1:
                    variance(1, b + 1)
                if s == 13:
                    normal(1, b + 1, 0)
                    normal(1, b + 1, 1)
                if s == 14:
                    ln_lo(1, b + 1, 0)
                    normal(1, b + 1, 2)
                    normal(1, b + 1, 3)
                if s == 15:
                    ln_lo(1, b + 1, 1)

            def attention(b):
                for s in range(H + 3):
                    first, second = slots(s)
                    for what, lag in DVE_STEP:
                        h = s - lag
                        if what == "first":
                            for tile in first:
                                proj_lo(b, tile)
                        elif what == "second":
                            for tile in second:
                                proj_lo(b, tile)
                        elif what == "norm":
                            if b + 1 < NB:
                                norm_step(b, s)
                        elif not 0 <= h < H:
                            pass
                        elif what == "max":
                            biased(b, h)
                        elif what == "1/sum a":
                            inverse(b, h, 1)
                        elif what == "1/sum b":
                            inverse(b, h, 0)
                        elif what == "lo":
                            e_hp.wait(e, (b, h))
                            e_lo.by(residue(ptl[h % 2][:, :], psB[:, 0:PW], pth[h % 2][:, :]), (b, h))
                        elif what == "add":
                            e_oc.wait(e, (b, h))
                            dst = o[64 * (h % 2):64 * (h % 2) + 64, h // 2, :]
                            e_oa.by(e.tensor_tensor(dst, psC[0:64, :], dst, ALU.add), (b, h))

            def split_lo(key, hi, lo, raw, scale):
                e_sh.wait(e, key)
                e_sl.by(e.scalar_tensor_tensor(lo, raw, scale, hi.bitcast(F32), ALU.mult, ALU.subtract), key)

            e_id.wait(e, "dist")
            e_x.wait(e, 0)
            for t in range(NT):
                stats(1, 0, t)
            variance(1, 0)
            for t in range(NT):
                normal(1, 0, t)
            for u in range(2):
                ln_lo(1, 0, u)
            for n in ("w1", "w2"):
                hi, lo, raw = SH[n]
                split_lo(n, hi[:, :, :], lo[:, :, :], raw[:, :, :], 0.5 if n == "w2" else 1.0)
            for h in range(H):
                split_lo(("q", h), wqh[:, :, qcols(h)], wql[:, :, qcols(h)], rawq[:, :, qcols(h)], q_scale(h))
            split_lo("kv", wqh[:, :, KV], wql[:, :, KV], rawq[:, :, KV], 1.0)
            split_lo("wout", woh[:, :, :], wol[:, :, :], rawo[:, :, :], 1.0)
            gelu_split(1, 0)
            for t in range(NT):
                add1(0, t)
            variance(2, 0)
            for t in range(NT):
                normal(2, 0, t)
            for u in range(2):
                ln_lo(2, 0, u)
            for tile in tiles_of(-1):
                proj_lo(0, tile)
            for b in B:
                more = b + 1 < NB
                attention(b)
                if more:
                    gelu_split(1, b + 1)
                out_lo(b, 0)
                out_lo(b, 1)
                add2(b, 0)
                out_lo(b, 2)
                add2(b, 1)
                out_lo(b, 3)
                add2(b, 2)
                add2(b, 3)
                variance(3, b)
                if more:
                    add1(b + 1, 0)
                normal(3, b, 0)
                normal(3, b, 1)
                if more:
                    add1(b + 1, 1)
                ln_lo(3, b, 0)
                normal(3, b, 2)
                normal(3, b, 3)
                if more:
                    add1(b + 1, 2)
                ln_lo(3, b, 1)
                if more:
                    add1(b + 1, 3)
                    variance(2, b + 1)
                gelu_split(2, b)
                if more:
                    normal(2, b + 1, 0)
                    normal(2, b + 1, 1)
                    ln_lo(2, b + 1, 0)
                    normal(2, b + 1, 2)
                    normal(2, b + 1, 3)
                add3(b, 0)
                if more:
                    ln_lo(2, b + 1, 1)
                for t in range(1, NT):
                    add3(b, t)
                if more:
                    for tile in tiles_of(-1):
                        proj_lo(b + 1, tile)

        @block.gpsimd
        def _(e):
            def power(L, b):
                e_ve.wait(e, (L, b))
                e_pw.by(e.tensor_tensor(rstd[:, L - 1, :], ve[:, L - 1, :], mhalf[:, :], ALU.pow), (L, b))

            def bias(L, b):
                e_xn.wait(e, (L, b, NT - 1))
                xs, bb = {1: (x0, b2h), 2: (x1, bo), 3: (x2, b2h)}[L]
                bb = bb[:, :].unsqueeze(1).broadcast_to([128, NT, D])
                e_pb.by(e.tensor_tensor(xs[:, :, :], xs[:, :, :], bb, ALU.add), (L, b))

            def attention(b):
                for s in range(H):
                    for i in QORDER:
                        e_rc.wait(e, (b, s, i // 2))
                        p = P[s % 2][:, QBASE[i]:QBASE[i] + 128 * (i + 1)]
                        e_nz.by(e.tensor_scalar(p, p, rs[:, s % 4, i:i + 1], 1.0, ALU.mult, ALU.mult), (b, s, i))
                    if b + 1 < NB:
                        if s == 12:
                            power(1, b + 1)
                        if s == 15:
                            bias(1, b + 1)

            e_id.by(e.memset(ident[:, :], 0.0), "zero")
            e_id.wait(e, "zero")
            e_id.by(e.affine_select(out=ident[:, :], in_=ident[:, :], compare_op=ALU.not_equal, fill=1.0,
                                    base=0, pattern=[[-1, 128]], channel_multiplier=1), "ident")
            e_id.by(e.iota(dist[:, :], [[1, T]], base=-(T - 128), channel_multiplier=-1,
                           allow_small_or_imprecise_dtypes=True), "iota")
            e_id.wait(e, "iota")
            e_id.by(e.affine_select(out=dist[:, :], in_=dist[:, :], compare_op=ALU.is_ge, fill=-BIG,
                                    base=T - 128, pattern=[[-1, T]], channel_multiplier=1), "dist")
            e_id.by(e.memset(mhalf[:, :], -0.5), "mhalf")
            e_id.wait(e, "mhalf")
            power(1, 0)
            e_w["b2"].wait(e, 0)
            e_sb.by(e.tensor_scalar(b2h[:, :], b2h[:, :], 0.5, 1.0, ALU.mult, ALU.mult), "b2")
            e_sb.wait(e, "b2")
            bias(1, 0)
            power(2, 0)
            e_w["bout"].wait(e, 0)
            bias(2, 0)
            for b in B:
                attention(b)
                power(3, b)
                bias(3, b)
                if b + 1 < NB:
                    power(2, b + 1)
                    bias(2, b + 1)


INPUTS = ["L0_attn_x", "L0_attn_w_qkv", "L0_attn_w_out", "L0_attn_b_out",
          "L0_ffn_w1", "L0_ffn_b1", "L0_ffn_w2", "L0_ffn_b2"]


def kernel(**inputs):
    import numpy as np
    import concourse.bacc as bacc
    from concourse import mybir
    from concourse.bass_utils import run_bass_kernel_spmd

    nc = bacc.Bacc("TRN2", target_bir_lowering=False, num_devices=1)
    arrays, args = {}, []
    for name in INPUTS:
        a = np.ascontiguousarray(inputs[name])
        arrays["in_" + name] = a
        args.append(nc.dram_tensor("in_" + name, a.shape, mybir.dt.from_np(a.dtype), kind="ExternalInput").ap())
    y = nc.dram_tensor("out_y", inputs["L0_attn_x"].shape, mybir.dt.float32, kind="ExternalOutput").ap()
    build(nc, *args, y)
    r = run_bass_kernel_spmd(nc, [arrays], core_ids=[0])
    return r.results[0]["out_y"]
```

```python
def build(nc, x_d, w_qkv_d, w_out_d, b_out_d, w1_d, b1_d, w2_d, b2_d, y_d):
    from concourse import mybir

    F32 = mybir.dt.float32
    F32R = mybir.dt.float32r
    I32 = mybir.dt.int32
    ALU = mybir.AluOpType
    ACT = mybir.ActivationFunctionType

    NB = x_d.shape[0]
    T, D, H, DH, F = 512, 256, 16, 64, 1024
    NT, NK, NM, NC = T // 128, D // 128, F // 128, H // 2
    EPS = 1e-5
    BIG = 3.0e38
    SLOPE = [2.0 ** (-0.5 * (h + 1)) for h in range(H)]
    BASE = {3: 0, 2: 512, 0: 896, 1: 1024}
    QBASE = BASE
    KBASE = {0: 0, 1: 512, 3: 896, 2: 1024}
    QORDER = (3, 2, 0, 1)
    PW = 1280
    PARTS = (slice(0, 512), slice(512, PW))

    at = [16512]

    def place(name, shape, dt, offset=None):
        n = 4
        for s in shape[1:]:
            n *= s
        if offset is None:
            offset = at[0]
            at[0] += -(-n // 32) * 32
        assert offset + n <= nc.sbuf_usable_end, name
        return nc.alloc_sbuf_tensor_at(name, list(shape), dt, offset=offset)

    w1h, w1l = place("w1h", [128, NK, F], F32R), place("w1l", [128, NK, F], F32R)
    w2h, w2l = place("w2h", [128, NM, D], F32R), place("w2l", [128, NM, D], F32R)
    wqh, wql = place("wqh", [128, NK, 3 * H * DH], F32R), place("wql", [128, NK, 3 * H * DH], F32R)
    woh, wol = place("woh", [128, NC, D], F32R), place("wol", [128, NC, D], F32R)
    dist = place("dist", [128, T], F32)
    ident = place("ident", [128, 128], F32)
    b2h = place("b2h", [128, D], F32)
    bo = place("bo", [128, D], F32)
    b1c = place("b1c", [128, NM], F32)
    mhalf = place("mhalf", [128, NT], F32)
    st = place("st", [128, 3, NT, 6], F32)
    mv = place("mv", [128, 3, NT, 2], F32)
    ve = place("ve", [128, 3, NT], F32)
    rstd = place("rstd", [128, 3, NT], F32)
    mx = place("mx", [128, 4, NT], F32)
    sm = place("sm", [128, 4, NT], F32)
    rs = place("rs", [128, 4, NT], F32)
    x0 = place("x0", [128, NT, D], F32)
    x1 = place("x1", [128, NT, D], F32)
    x2 = place("x2", [128, NT, D], F32)
    xn = place("xn", [128, 2, D], F32)
    xth, xtl = place("xth", [128, NK, T], F32R), place("xtl", [128, NK, T], F32R)
    at_o = at[0]
    o = place("o", [128, NC, T], F32)

    R = at[0]
    qk = place("qk", [128, 4, T], F32R, R)
    stack = [place(f"stack{i}", [128, 3, T], F32R, R + 8192 + 6144 * i) for i in range(2)]
    v = [place(f"v{i}", [128, NT, 4, 128], F32R, R + 20480 + 8192 * i) for i in range(2)]
    P = [place(f"P{i}", [128, PW], F32, R + 36864 + 4 * PW * i) for i in range(2)]
    pth = [place(f"pth{i}", [128, PW], F32R, R + 47104 + 8 * PW * i) for i in range(2)]
    ptl = [place(f"ptl{i}", [128, PW], F32R, R + 47104 + 4 * PW + 8 * PW * i) for i in range(2)]
    g_at = {1: [0, 4096, 8192, 12288, 22528, 47104, 51200, 55296],
            2: [28672, 32768] + [41984 + 4096 * m for m in range(NM - 2)]}
    gh = {f: [place(f"gh{f}{m}", [128, T], F32R, R + a) for m, a in enumerate(g_at[f])] for f in (1, 2)}
    gl = {f: [place(f"gl{f}{m}", [128, T], F32R, R + a + 2048) for m, a in enumerate(g_at[f])] for f in (1, 2)}
    o_at = (28672, 36864, 59392)
    oh = [place(f"oh{i}", [128, NC, 128], F32R, R + a) for i, a in enumerate(o_at)]
    ol = [place(f"ol{i}", [128, NC, 128], F32R, R + a + 4096) for i, a in enumerate(o_at)]
    gt = place("gt", [128, 3, T], F32, R + 16384)
    raw1 = place("raw1", [128, NK, F], F32, at_o)
    raw2 = place("raw2", [128, NM, D], F32, at_o + 8192)
    rawq = place("rawq", [128, NK, H * DH], F32, R + 26624)
    rawk = place("rawk", [128, NK, H * DH], F32, R + 34816)
    rawv = place("rawv", [128, NK, H * DH], F32, at_o)
    rawo = place("rawo", [128, NC, D], F32, at_o + 8192)

    psA = nc.alloc_psum_tensor("psA", [128, 3 * 512], F32)
    psB = nc.alloc_psum_tensor("psB", [128, 3 * 512], F32)
    psC = nc.alloc_psum_tensor("psC", [128, 512], F32)
    psD = nc.alloc_psum_tensor("psD", [128, 512], F32)

    def bk(i):
        if i < 3:
            return psA[:, 512 * i:512 * i + 512]
        if i < 6:
            return psB[:, 512 * (i - 3):512 * (i - 3) + 512]
        return (psC if i == 6 else psD)[:, :]

    PE_STEP = [("scores", 0), ("first", 0), ("up a", 0), ("norm", 0), ("transposes", 1), ("second", 0),
               ("up b", 0), ("values", 2)]
    ACT_STEP = [("half", 3), ("up a", 0), ("exp 0", 0), ("norm", 0), ("exp 1", 0), ("first", 0), ("hi 0", 1),
                ("hi 1", 1), ("up b", 0), ("exp 2", 0), ("second", 0), ("exp 3", 0)]
    DVE_STEP = [("max 0", 0), ("max 1", 0), ("max 2", 0), ("max 3", 0), ("add", 3), ("1/sum a", 0), ("up a", 0),
                ("norm", 0), ("first", 0), ("lo 0", 1), ("lo 1", 1), ("up b", 0), ("second", 0), ("1/sum b", 0)]
    OUT_BANK = (3, 4, 7, 3)
    UPS = {(H, "up a"): [0, 1], (H, "up b"): [2, 3], (H + 1, "up b"): [4]}
    EARLY = 5

    B = range(NB)
    ffn = [(1, 0)] + [e for b in B for e in ([(1, b + 1)] if b + 1 < NB else []) + [(2, b)]]
    lns = [(1, 0), (2, 0)] + [e for b in B for e in (
        [(1, b + 1), (3, b), (2, b + 1)] if b + 1 < NB else [(3, b)])]

    def tiles_of(s):
        if s == -1:
            return [("k", 0), ("q", 0), ("v", 0, 0)]
        c, odd = divmod(s, 2)
        if odd:
            g, u = divmod(c + 1, 2)
            return [("v", g, u)] if g < 4 else []
        return [("k", c + 1), ("q", c + 1)] if c + 1 < NC else []

    def slots(s):
        t = tiles_of(s) if s < H else []
        return (t[:1], t[1:]) if s % 2 == 0 else ([], t)

    def step_uses(s):
        first, second = slots(s)
        uses = []
        for what, lag in PE_STEP:
            if what == "first":
                uses += first
            elif what == "second":
                uses += second
            elif what == "norm" and H - 2 <= s < H:
                uses.append(("norm", s - (H - 2)))
            elif what == "values" and 0 <= s - lag < H:
                uses.append(("values", s - lag))
        return uses

    ring = [("v", 0, 0)] + [u for s in range(H + 3) for u in step_uses(s)]

    def bank_of(use):
        if use in (("q", 0), ("k", 0)):
            return 0 if use[0] == "q" else 1
        return 7 - ring.index(use) % 2

    tiles = [t for s in range(-1, H) for t in tiles_of(s)]
    heads = [(b, h) for b in B for h in range(H)]
    per_part = [(b, h, part) for b, h in heads for part in range(2)]
    per_block = [(b, h, i) for b, h in heads for i in QORDER]
    units = [(L, b, u) for L, b in lns for u in range(2)]
    rows = [(L, b, t) for L, b in lns for t in range(NT)]
    hidden = [(f, b, m) for f, b in ffn for m in range(NM)]
    down = [(f, b, t) for f, b in ffn for t in range(NT)]
    outs = [(b, t) for b in B for t in range(NT)]
    proj = [(b, t) for b in B for t in tiles]

    class Events:
        def __init__(self, name, keys, step=1):
            self.sem, self.step, self.made = nc.alloc_semaphore(name), step, 0
            self.keys = list(keys)
            self.value = {k: step * (n + 1) for n, k in enumerate(self.keys)}

        def by(self, instruction, key):
            assert self.keys[self.made] == key, (self.sem, key, self.keys[self.made])
            self.made += 1
            instruction.then_inc(self.sem, self.step)

        def wait(self, engine, key):
            engine.wait_ge(self.sem, self.value[key])

    e_qk = Events("qk_done", per_block)
    e_tp = Events("tp_done", per_part)
    e_pv = Events("pv_done", heads)
    e_pj = Events("pj_done", proj)
    e_lt = Events("lt_done", units)
    e_up = Events("up_done", hidden)
    e_dn = Events("dn_done", down)
    e_ot = Events("ot_done", outs)
    e_ex = Events("ex_done", per_block)
    e_hp = Events("hp_done", per_part)
    e_oc = Events("oc_done", heads)
    e_ph = Events("ph_done", proj)
    e_lh = Events("lh_done", units)
    e_gl = Events("gl_done", hidden)
    e_oh = Events("oh_done", outs)
    e_tt = Events("tt_done", per_block)
    e_rc = Events("rc_done", [(b, h, half) for b, h in heads for half in (1, 0)])
    e_lo = Events("lo_done", per_part)
    e_oa = Events("oa_done", heads)
    e_pl = Events("pl_done", proj)
    e_ll = Events("ll_done", units)
    e_gh = Events("gh_done", hidden)
    e_gs = Events("gs_done", hidden)
    e_ol = Events("ol_done", outs)
    e_r1 = Events("r1_done", [(f, b, t) for f, b, t in down if f == 1])
    e_r3 = Events("r3_done", [(f, b, t) for f, b, t in down if f == 2])
    e_r2 = Events("r2_done", outs)
    e_bs = Events("bs_done", rows)
    e_ba = Events("ba_done", rows)
    e_ve = Events("ve_done", lns)
    e_xn = Events("xn_done", rows)
    e_nz = Events("nz_done", per_block)
    e_pw = Events("pw_done", lns)
    e_pb = Events("pb_done", lns)
    e_x = Events("x_in", list(B), 16)
    e_y = Events("y_out", list(B), 16)
    e_sq = [Events(f"stack_q{i}", [(b, h, n) for b, h in heads if h % 2 == i for n in range(2)], 16)
            for i in range(2)]
    e_sk = [Events(f"stack_k{i}", [(b, h, n) for b, h in heads if h % 2 == i for n in range(2)], 16)
            for i in range(2)]
    names = ["w1a", "w1b", "b1", "w2", "b2", "wq", "wk", "wv", "wout", "bout"]
    e_w = {n: Events("in_" + n, [0], 16) for n in names}
    e_sh = Events("set_hi", ["w1a", "w1b", "w2"] + [("q", h) for h in range(H)] + ["wk", "wv", "wout"])
    e_sl = Events("set_lo", ["w1a", "w1b", "w2"] + [("q", h) for h in range(H)] + ["wk", "wv", "wout"])
    e_sb = Events("set_bias", ["b2"])
    e_id = Events("set_ident", ["zero", "ident", "iota", "dist", "mhalf"])

    def ln_bank(L, b, u):
        return bk(bank_of(("norm", u)) if L == 1 and b > 0 else 3 + u)

    def ring_free(e, b, use):
        n = ring.index(use)
        if n >= 2:
            before, pb = ring[n - 2], b
        elif n == 1:
            (e_r3 if b > 0 else e_r1).wait(e, (2, b - 1, NT - 1) if b > 0 else (1, 0, NT - 1))
            return
        elif b > 0:
            e_oa.wait(e, (b - 1, H - 1))
            e_ll.wait(e, (1, b, 1))
            e_r2.wait(e, (b - 1, 2))
            return
        else:
            return
        if before[0] == "values":
            e_oa.wait(e, (pb, before[1]))
        elif before[0] == "norm":
            if pb + 1 < NB:
                e_ll.wait(e, (1, pb + 1, before[1]))
        else:
            e_pl.wait(e, (pb, before))

    HD = H * DH
    KC, VC = slice(HD, 2 * HD), slice(2 * HD, 3 * HD)
    FH = F // 2
    SH = {"w1a": (w1h[:, :, 0:FH], w1l[:, :, 0:FH], raw1[:, :, 0:FH]),
          "w1b": (w1h[:, :, FH:F], w1l[:, :, FH:F], raw1[:, :, FH:F]),
          "w2": (w2h[:, :, :], w2l[:, :, :], raw2[:, :, :]),
          "wk": (wqh[:, :, KC], wql[:, :, KC], rawk[:, :, :]), "wv": (wqh[:, :, VC], wql[:, :, VC], rawv[:, :, :]),
          "wout": (woh[:, :, :], wol[:, :, :], rawo[:, :, :])}

    def qcols(h):
        return slice(h * DH, (h + 1) * DH)

    def q_scale(h):
        return DH ** -0.5 / SLOPE[h]

    block = nc.Block()
    with block:
        @block.sync
        def _(e):
            def load_x(b):
                if b > 0:
                    e_r1.wait(e, (1, b - 1, NT - 1))
                e_x.by(e.dma_start(x0[:, :, :], x_d[b].rearrange("(t p) n -> p t n", p=128)), b)

            def load_qkv(n, dst, part):
                src = w_qkv_d[:, part * HD:(part + 1) * HD].rearrange("(k p) n -> p k n", p=128)
                e_w[n].by(e.dma_start(dst[:, :, :], src), 0)

            load_x(0)
            for n, cs in (("w1a", slice(0, FH)), ("w1b", slice(FH, F))):
                e_w[n].by(e.dma_start(raw1[:, :, cs], w1_d[:, cs].rearrange("(k p) n -> p k n", p=128)), 0)
            e_w["b1"].by(e.dma_start(b1c[:, :], b1_d.rearrange("(m p) -> p m", p=128),
                                     allow_slow_non_contiguous=True), 0)
            e_w["w2"].by(e.dma_start(raw2[:, :, :], w2_d.rearrange("(m p) n -> p m n", p=128)), 0)
            e_w["b2"].by(e.dma_start(b2h[:, :], b2_d.partition_broadcast(128)), 0)
            load_qkv("wq", rawq, 0)
            load_qkv("wk", rawk, 1)
            e_sl.wait(e, "w1b")
            load_qkv("wv", rawv, 2)
            e_sl.wait(e, "w2")
            e_w["wout"].by(e.dma_start(rawo[:, :, :], w_out_d.rearrange("(c p) n -> p c n", p=128)), 0)
            e_w["bout"].by(e.dma_start(bo[:, :], b_out_d.partition_broadcast(128)), 0)

            def store_y(b):
                e_r3.wait(e, (2, b, NT - 1))
                e_y.by(e.dma_start(y_d[b].rearrange("(t p) n -> p t n", p=128), x2[:, :, :]), b)

            def stack_head(b, h):
                c, i = h // 2, h % 2
                src = qk[64 * i:64 * i + 64, :, :].bitcast(F32)
                dst = stack[i]
                n = heads.index((b, h))
                e_pl.wait(e, (b, ("k", c)))
                if n >= 2:
                    e_qk.wait(e, (*heads[n - 2], QORDER[-1]))
                for half in range(2):
                    e_sk[i].by(e.dma_start(dst[64 * half:64 * half + 64, 1:3, :].bitcast(F32), src[:, 1:3, :]),
                               (b, h, half))
                e_pl.wait(e, (b, ("q", c)))
                e_sq[i].by(e.dma_start(dst[0:64, 0, :].bitcast(F32), src[:, 0, :]), (b, h, 0))
                e_sq[i].by(e.dma_start(dst[64:128, 0, :].bitcast(F32), src[:, 3, :]), (b, h, 1))

            stack_head(0, 0)
            stack_head(0, 1)
            for b in B:
                for h in range(2, H):
                    if h == 4 and b > 0:
                        store_y(b - 1)
                    if h == 6 and b + 1 < NB:
                        load_x(b + 1)
                    stack_head(b, h)
                if b + 1 < NB:
                    stack_head(b + 1, 0)
                    stack_head(b + 1, 1)
            store_y(NB - 1)
            e_y.wait(e, NB - 1)

        @block.tensor
        def _(e):
            def mm(out, lhsT, rhs, first, last):
                return e.matmul(out, lhsT, rhs, start=first, stop=last)

            def three(out, pairs):
                n = len(pairs)
                for i, (ah, al, bh, bl) in enumerate(pairs):
                    mm(out, ah, bh, i == 0, False)
                    mm(out, ah, bl, False, False)
                    inst = mm(out, al, bh, False, i == n - 1)
                return inst

            def ln_transpose(L, b, u):
                dst = ln_bank(L, b, u)
                n = units.index((L, b, u))
                if L == 1:
                    if b > 0:
                        ring_free(e, b - 1, ("norm", u))
                elif L == 3:
                    e_r2.wait(e, (b, 2 + u))
                elif b > 0:
                    e_ll.wait(e, (3, b - 1, u))
                for t in (2 * u, 2 * u + 1):
                    e_xn.wait(e, (L, b, t))
                    for k in range(NK):
                        col = k * 256 + (t - 2 * u) * 128
                        last = e.transpose(dst[:, col:col + 128], xn[:, t % 2, k * 128:(k + 1) * 128], ident[:, :])
                e_lt.by(last, (L, b, u))

            def up(f, b, ms):
                L = 1 if f == 1 else 3
                if 0 in ms:
                    e_ll.wait(e, (L, b, 1))
                    if f == 1 and b > 0:
                        e_tt.wait(e, (b - 1, H - 1, QORDER[-1]))
                    if f == 2 and b + 1 < NB:
                        e_gl.wait(e, (1, b + 1, NM - 1))
                    if f == 2 and b + 1 == NB:
                        e_tt.wait(e, (b, H - 1, QORDER[-1]))
                for m in ms:
                    if m >= 3:
                        e_gl.wait(e, (f, b, m - 3))
                    cs = slice(m * 128, m * 128 + 128)
                    last = three(bk(m % 3), [(w1h[:, k, cs], w1l[:, k, cs], xth[:, k, :], xtl[:, k, :])
                                             for k in range(NK)])
                    e_up.by(last, (f, b, m))

            def dn(f, b, t):
                if t >= 2:
                    (e_r1 if f == 1 else e_r3).wait(e, (f, b, t - 2))
                elif f == 1 and b > 0:
                    e_lo.wait(e, (b - 1, H - 1, 1))
                    e_oa.wait(e, (b - 1, H - 1))
                elif f == 2 and b + 1 < NB:
                    e_r1.wait(e, (1, b + 1, NT - 2 + t))
                elif f == 2:
                    e_lo.wait(e, (b, H - 1, 1))
                    e_oa.wait(e, (b, H - 1))
                ts = slice(t * 128, t * 128 + 128)
                dst = bk(5 + t % 2)[:, 0:D]
                for m in range(NM):
                    if t == 0:
                        e_gs.wait(e, (f, b, m))
                    g, l, wh, wl = gh[f][m][:, ts], gl[f][m][:, ts], w2h[:, m, :], w2l[:, m, :]
                    mm(dst, g, wh, m == 0, False)
                    mm(dst, g, wl, False, False)
                    last = mm(dst, l, wh, False, m == NM - 1)
                e_dn.by(last, (f, b, t))

            def out_proj(b, t):
                if (b, t) == (0, 0):
                    e_sl.wait(e, "wout")
                if t == 3:
                    e_r2.wait(e, (b, 0))
                elif t == 0:
                    e_lo.wait(e, (b, H - 1, 1))
                e_ol.wait(e, (b, t))
                i = t % 3
                last = three(bk(OUT_BANK[t])[:, 0:D], [(oh[i][:, c, :], ol[i][:, c, :], woh[:, c, :], wol[:, c, :])
                                               for c in range(NC)])
                e_ot.by(last, (b, t))

            def proj_tile(b, tile):
                dst = bk(bank_of(tile))
                if tile == tiles[0]:
                    e_ll.wait(e, (2, b, 1))
                    e_gl.wait(e, (2, b - 1, NM - 1) if b > 0 else (1, 0, NM - 1))
                if tile not in tiles[:2]:
                    ring_free(e, b, tile)
                if tile[0] == "v":
                    _, g, u = tile
                    gs = slice(2 * HD + g * 256, 2 * HD + g * 256 + 256)
                    for j in range(2):
                        ts = slice((2 * u + j) * 128, (2 * u + j) * 128 + 128)
                        last = three(dst[:, j * 256:j * 256 + 256],
                                     [(xth[:, k, ts], xtl[:, k, ts], wqh[:, k, gs], wql[:, k, gs])
                                      for k in range(NK)])
                else:
                    kind, c = tile
                    cs = slice((HD if kind == "k" else 0) + c * 128, (HD if kind == "k" else 0) + c * 128 + 128)
                    last = three(dst, [(wqh[:, k, cs], wql[:, k, cs], xth[:, k, :], xtl[:, k, :])
                                       for k in range(NK)])
                e_pj.by(last, (b, tile))

            def scores(b, h):
                n = heads.index((b, h))
                sk = stack[h % 2]
                e_sq[h % 2].wait(e, (b, h, 1))
                e_sk[h % 2].wait(e, (b, h, 1))
                if h == 0 and b > 0:
                    e_gl.wait(e, (2, b - 1, NM - 1))
                for i in QORDER:
                    if n > 0:
                        e_tt.wait(e, (*heads[n - 1], 0 if i == 2 else i))
                    w = 128 * (i + 1)
                    dst = psA[:, QBASE[i]:QBASE[i] + w]
                    qs = sk[:, 0, i * 128:i * 128 + 128]
                    mm(dst, qs, sk[:, 1, 0:w], True, False)
                    e_qk.by(mm(dst, qs, sk[:, 2, 0:w], False, True), (b, h, i))

            def transposes(b, h):
                n = heads.index((b, h))
                if h == 0 and b > 0:
                    e_ll.wait(e, (2, b, 1))
                    e_r3.wait(e, (2, b - 1, NT - 2))
                e_nz.wait(e, (b, h, QORDER[-1]))
                for j in range(NT):
                    if n > 0 and j < 2:
                        e_lo.wait(e, (*heads[n - 1], j))
                    for i in range(j, NT):
                        src = P[h % 2][:, QBASE[i] + 128 * j:QBASE[i] + 128 * j + 128]
                        col = KBASE[j] + 128 * (i - j)
                        last = e.transpose(psB[:, col:col + 128], src, ident[:, :])
                    if j == 0:
                        e_tp.by(last, (b, h, 0))
                e_tp.by(last, (b, h, 1))

            def values(b, h):
                ring_free(e, b, ("values", h))
                pv = bk(bank_of(("values", h)))
                e_pl.wait(e, (b, ("v", h // 4, 1)))
                vv = v[(h // 4) % 2]
                for j in range(NT):
                    w = T - 128 * j
                    ks = slice(KBASE[j], KBASE[j] + w)
                    lhs = vv[:, j, h % 4, :]
                    if j < 2:
                        e_lo.wait(e, (b, h, j))
                    mm(pv[:, 128 * j:T], lhs, pth[h % 2][:, ks], j == 0, False)
                    last = mm(pv[:, 128 * j:T], lhs, ptl[h % 2][:, ks], False, j == NT - 1)
                e_pv.by(last, (b, h))

            def attention(b):
                if b == 0:
                    proj_tile(b, tiles[2])
                scores(b, 0)
                if b > 0:
                    dn(2, b - 1, 3)
                    proj_tile(b, tiles[2])
                for s in range(H + 3):
                    first, second = slots(s)
                    for what, lag in PE_STEP:
                        h = s - lag
                        if what == "first":
                            for tile in first:
                                proj_tile(b, tile)
                        elif what == "second":
                            for tile in second:
                                proj_tile(b, tile)
                        elif what == "norm":
                            if H - 2 <= s < H and b + 1 < NB:
                                ln_transpose(1, b + 1, s - (H - 2))
                        elif what in ("up a", "up b"):
                            if b + 1 < NB:
                                up(1, b + 1, UPS.get((s, what), []))
                        elif 0 <= h < H and s > 0:
                            {"scores": scores, "transposes": transposes, "values": values}[what](b, h)

            e_id.wait(e, "ident")
            for u in range(2):
                ln_transpose(1, 0, u)
            e_sl.wait(e, "w1a")
            up(1, 0, range(NM // 2))
            e_sl.wait(e, "w1b")
            up(1, 0, range(NM // 2, NM))
            e_sl.wait(e, "w2")
            for t in range(NT):
                dn(1, 0, t)
            for u in range(2):
                ln_transpose(2, 0, u)
            e_sl.wait(e, "wv")
            for tile in tiles[:2]:
                proj_tile(0, tile)
            for b in B:
                more = b + 1 < NB
                attention(b)
                if more:
                    up(1, b + 1, range(EARLY, NM))
                for t in range(NT):
                    out_proj(b, t)
                if more:
                    dn(1, b + 1, 0)
                    dn(1, b + 1, 1)
                ln_transpose(3, b, 0)
                if more:
                    dn(1, b + 1, 2)
                ln_transpose(3, b, 1)
                if more:
                    dn(1, b + 1, 3)
                up(2, b, range(5))
                if more:
                    ln_transpose(2, b + 1, 0)
                up(2, b, range(5, 7))
                if more:
                    ln_transpose(2, b + 1, 1)
                up(2, b, range(7, NM))
                dn(2, b, 0)
                if more:
                    for tile in tiles[:2]:
                        proj_tile(b + 1, tile)
                dn(2, b, 1)
                dn(2, b, 2)
            dn(2, NB - 1, 3)

        def tile_parts(tile, dst_lo):
            if tile[0] == "v":
                _, g, u = tile
                o64 = 64 if dst_lo else 0
                return (v[g % 2][:, 2 * u:2 * u + 2, :, o64:o64 + 64],
                        bk(bank_of(tile)).rearrange("p (t h d) -> p t h d", t=2, h=4))
            plane = {"q": (0, 3), "k": (1, 2)}[tile[0]][1 if dst_lo else 0]
            return qk[:, plane, :], bk(bank_of(tile))

        @block.scalar
        def _(e):
            def proj_hi(b, tile):
                e_pj.wait(e, (b, tile))
                if tile[0] in "qk":
                    c = tile[1]
                    if (b, c) != (0, 0):
                        pb, pc = (b, c - 1) if c else (b - 1, NC - 1)
                        for i, stacked in enumerate(e_sq if tile[0] == "q" else e_sk):
                            stacked.wait(e, (pb, 2 * pc + i, 1))
                elif tile[1] < 2:
                    if b > 0:
                        e_pv.wait(e, (b - 1, H - 1))
                else:
                    e_pv.wait(e, (b, 4 * tile[1] - 5))
                dst, src = tile_parts(tile, False)
                e_ph.by(e.activation(dst, src, ACT.Copy), (b, tile))

            def ln_hi(L, b, u):
                e_lt.wait(e, (L, b, u))
                if L == 1 and b > 0:
                    e_pj.wait(e, (b - 1, tiles[-1]))
                if L == 2:
                    e_up.wait(e, (2, b - 1, NM - 1) if b > 0 else (1, 0, NM - 1))
                if L == 3 and b + 1 < NB:
                    e_up.wait(e, (1, b + 1, NM - 1))
                us = slice(256 * u, 256 * u + 256)
                e_lh.by(e.activation(xth[:, :, us], ln_bank(L, b, u).rearrange("p (k n) -> p k n", k=2), ACT.Copy),
                        (L, b, u))

            def gelu(f, b, ms):
                n0 = hidden.index((f, b, 0))
                for m in ms:
                    e_up.wait(e, (f, b, m))
                    if n0 + m >= 3:
                        e_gs.wait(e, hidden[n0 + m - 3])
                    e_gl.by(e.activation(gt[:, m % 3, :], bk(m % 3), ACT.Gelu, bias=b1c[:, m:m + 1]), (f, b, m))

            def out_hi(b, t):
                if t == 0:
                    e_oa.wait(e, (b, H - 1))
                if t == 3:
                    e_ot.wait(e, (b, 0))
                e_oh.by(e.activation(oh[t % 3][:, :, :], o[:, :, 128 * t:128 * t + 128], ACT.Copy), (b, t))

            def exps(b, h, blocks):
                for i in blocks:
                    e_tt.wait(e, (b, h, i))
                    p = P[h % 2][:, QBASE[i]:QBASE[i] + 128 * (i + 1)]
                    r = h % 4
                    e_ex.by(e.activation(p, p, ACT.Exp, bias=mx[:, r, i:i + 1], scale=-1.0,
                                         accum_out=sm[:, r, i:i + 1]), (b, h, i))

            def attention(b):
                if b == 0:
                    proj_hi(b, tiles[2])
                exps(b, 0, QORDER)
                if b > 0:
                    proj_hi(b, tiles[2])
                for s in range(H + 3):
                    first, second = slots(s)
                    for what, lag in ACT_STEP:
                        h = s - lag
                        if what == "first":
                            for tile in first:
                                proj_hi(b, tile)
                        elif what == "second":
                            for tile in second:
                                proj_hi(b, tile)
                        elif what == "norm":
                            if H - 2 <= s < H and b + 1 < NB:
                                ln_hi(1, b + 1, s - (H - 2))
                        elif what in ("up a", "up b"):
                            if b + 1 < NB:
                                gelu(1, b + 1, UPS.get((s, what), []))
                        elif not 0 <= h < H or s == 0:
                            pass
                        elif what[:3] == "exp":
                            exps(b, h, [QORDER[int(what[4])]])
                        elif what[:2] == "hi":
                            part = int(what[3])
                            e_tp.wait(e, (b, h, part))
                            if h >= 2:
                                e_pv.wait(e, (b, h - 2))
                            ps = PARTS[part]
                            e_hp.by(e.activation(pth[h % 2][:, ps], psB[:, ps], ACT.Copy), (b, h, part))
                        elif what == "half":
                            e_pv.wait(e, (b, h))
                            src = bk(bank_of(("values", h)))[64:128, :]
                            dst = o[64 * (h % 2):64 * (h % 2) + 64, h // 2, :]
                            e_oc.by(e.activation(dst, src, ACT.Copy), (b, h))

            def split_hi(key, dst, src, scale):
                e_sh.by(e.activation(dst, src, ACT.Copy, scale=scale), key)

            def split_weight_hi(n):
                e_w[n].wait(e, 0)
                if n == "wq":
                    for h in range(H):
                        split_hi(("q", h), wqh[:, :, qcols(h)], rawq[:, :, qcols(h)], q_scale(h))
                else:
                    split_hi(n, SH[n][0], SH[n][2], 0.5 if n == "w2" else 1.0)

            split_weight_hi("w1a")
            split_weight_hi("w1b")
            for u in range(2):
                ln_hi(1, 0, u)
            e_w["b1"].wait(e, 0)
            gelu(1, 0, range(2))
            split_weight_hi("w2")
            gelu(1, 0, range(2, NM))
            for n in ("wq", "wk", "wv", "wout"):
                split_weight_hi(n)
            for u in range(2):
                ln_hi(2, 0, u)
            for tile in tiles[:2]:
                proj_hi(0, tile)
            for b in B:
                more = b + 1 < NB
                attention(b)
                if more:
                    gelu(1, b + 1, range(EARLY, EARLY + 1))
                out_hi(b, 0)
                if more:
                    gelu(1, b + 1, range(EARLY + 1, EARLY + 2))
                out_hi(b, 1)
                out_hi(b, 2)
                if more:
                    gelu(1, b + 1, range(EARLY + 2, NM))
                out_hi(b, 3)
                for u in range(2):
                    ln_hi(3, b, u)
                gelu(2, b, range(NM))
                if more:
                    for u in range(2):
                        ln_hi(2, b + 1, u)
                    for tile in tiles[:2]:
                        proj_hi(b + 1, tile)

        @block.vector
        def _(e):
            xs = {1: x0, 2: x1, 3: x2}

            def residue(dst, src, hi):
                return e.tensor_tensor(dst, src, hi.bitcast(F32), ALU.subtract)

            def proj_lo(b, tile):
                e_ph.wait(e, (b, tile))
                dst, src = tile_parts(tile, True)
                hi, _ = tile_parts(tile, False)
                e_pl.by(residue(dst, src, hi), (b, tile))

            def ln_lo(L, b, u):
                e_lh.wait(e, (L, b, u))
                us = slice(256 * u, 256 * u + 256)
                e_ll.by(residue(xtl[:, :, us], ln_bank(L, b, u).rearrange("p (k n) -> p k n", k=2), xth[:, :, us]),
                        (L, b, u))

            def stats(L, b, t):
                e_bs.by(e.bn_stats(st[:, L - 1, t, :], xs[L][:, t, :]), (L, b, t))
                e_bs.wait(e, (L, b, t))
                e_ba.by(e.bn_aggr(mv[:, L - 1, t, :], st[:, L - 1, t, :]), (L, b, t))

            def variance(L, b):
                e_ba.wait(e, (L, b, NT - 1))
                e_ve.by(e.tensor_scalar(ve[:, L - 1, :], mv[:, L - 1, :, 1], EPS, None, ALU.add), (L, b))

            def normal(L, b, t):
                if t == 0:
                    e_pw.wait(e, (L, b))
                    n = lns.index((L, b))
                    if n > 0:
                        e_lt.wait(e, (*lns[n - 1], 1))
                if t == 2:
                    e_lt.wait(e, (L, b, 0))
                e_xn.by(e.tensor_scalar(xn[:, t % 2, :], xs[L][:, t, :], mv[:, L - 1, t, 0:1], rstd[:, L - 1, t:t + 1],
                                        ALU.subtract, ALU.mult), (L, b, t))

            def add(events, key, produced, pkey, dst, other, L, b, t):
                produced.wait(e, pkey)
                e_pb.wait(e, (L, b))
                src = bk(5 + t % 2) if produced is e_dn else bk(OUT_BANK[t])
                events.by(e.tensor_tensor(dst[:, t, :], src[:, 0:D], other[:, t, :], ALU.add), key)
                events.wait(e, key)

            def add1(b, t):
                if t == 0 and b > 0:
                    e_r2.wait(e, (b - 1, NT - 1))
                add(e_r1, (1, b, t), e_dn, (1, b, t), x1, x0, 1, b, t)
                stats(2, b, t)

            def add2(b, t):
                if t == 0 and b > 0:
                    e_y.wait(e, b - 1)
                add(e_r2, (b, t), e_ot, (b, t), x2, x1, 2, b, t)
                stats(3, b, t)

            def add3(b, t):
                add(e_r3, (2, b, t), e_dn, (2, b, t), x2, x2, 3, b, t)

            def gelu_split(f, b, ms):
                for m in ms:
                    e_gl.wait(e, (f, b, m))
                    e_gh.by(e.tensor_copy(gh[f][m][:, :], gt[:, m % 3, :]), (f, b, m))
                    e_gh.wait(e, (f, b, m))
                    e_gs.by(residue(gl[f][m][:, :], gt[:, m % 3, :], gh[f][m][:, :]), (f, b, m))

            def out_lo(b, t):
                e_oh.wait(e, (b, t))
                e_ol.by(residue(ol[t % 3][:, :, :], o[:, :, 128 * t:128 * t + 128], oh[t % 3][:, :, :]), (b, t))

            def inverse(b, h, half):
                e_ex.wait(e, (b, h, 2 if half else 1))
                cs = slice(2 * half, 2 * half + 2)
                e_rc.by(e.reciprocal(rs[:, h % 4, cs], sm[:, h % 4, cs]), (b, h, half))

            def biased(b, h, n):
                for i in [QORDER[n]]:
                    e_qk.wait(e, (b, h, 0 if i == 2 else i))
                    if n == 0 and h >= 2:
                        e_tp.wait(e, (b, h - 2, 1))
                    w = 128 * (i + 1)
                    cs = slice(QBASE[i], QBASE[i] + w)
                    e_tt.by(e.tensor_tensor_reduce(
                        out=P[h % 2][:, cs], in0=psA[:, cs], in1=dist[:, T - w:T], scale=-SLOPE[h],
                        scalar=BIG, op0=ALU.add, op1=ALU.min, accum_out=mx[:, h % 4, i:i + 1]), (b, h, i))

            def norm_step(b, s):
                if s == 9:
                    e_x.wait(e, b + 1)
                if 9 <= s < 9 + NT:
                    stats(1, b + 1, s - 9)
                if s == 9 + NT - 1:
                    variance(1, b + 1)
                if s == 13:
                    normal(1, b + 1, 0)
                    normal(1, b + 1, 1)
                if s == 14:
                    ln_lo(1, b + 1, 0)
                    normal(1, b + 1, 2)
                    normal(1, b + 1, 3)
                if s == 15:
                    ln_lo(1, b + 1, 1)

            def attention(b):
                if b == 0:
                    proj_lo(b, tiles[2])
                for n in range(NT):
                    biased(b, 0, n)
                if b == 0:
                    split_weight_lo("wout")
                inverse(b, 0, 1)
                inverse(b, 0, 0)
                if b > 0:
                    add3(b - 1, 3)
                    proj_lo(b, tiles[2])
                for s in range(H + 3):
                    first, second = slots(s)
                    for what, lag in DVE_STEP:
                        h = s - lag
                        if what == "first":
                            for tile in first:
                                proj_lo(b, tile)
                        elif what == "second":
                            for tile in second:
                                proj_lo(b, tile)
                        elif what == "norm":
                            if b + 1 < NB:
                                norm_step(b, s)
                        elif what in ("up a", "up b"):
                            if b + 1 < NB:
                                gelu_split(1, b + 1, UPS.get((s, what), []))
                        elif not 0 <= h < H or s == 0:
                            pass
                        elif what[:3] == "max":
                            biased(b, h, int(what[4]))
                        elif what == "1/sum a":
                            inverse(b, h, 1)
                        elif what == "1/sum b":
                            inverse(b, h, 0)
                        elif what[:2] == "lo":
                            part = int(what[3])
                            ps = PARTS[part]
                            e_hp.wait(e, (b, h, part))
                            e_lo.by(residue(ptl[h % 2][:, ps], psB[:, ps], pth[h % 2][:, ps]), (b, h, part))
                        elif what == "add":
                            e_oc.wait(e, (b, h))
                            dst = o[64 * (h % 2):64 * (h % 2) + 64, h // 2, :]
                            e_oa.by(e.tensor_tensor(dst, bk(bank_of(("values", h)))[0:64, :], dst, ALU.add), (b, h))

            def split_lo(key, hi, lo, raw, scale):
                e_sh.wait(e, key)
                e_sl.by(e.scalar_tensor_tensor(lo, raw, scale, hi.bitcast(F32), ALU.mult, ALU.subtract), key)

            def split_weight_lo(n):
                if n == "wq":
                    for h in range(H):
                        split_lo(("q", h), wqh[:, :, qcols(h)], wql[:, :, qcols(h)], rawq[:, :, qcols(h)], q_scale(h))
                else:
                    split_lo(n, *SH[n], 0.5 if n == "w2" else 1.0)

            e_x.wait(e, 0)
            for t in range(NT):
                stats(1, 0, t)
            variance(1, 0)
            split_weight_lo("w1a")
            for t in range(NT):
                normal(1, 0, t)
            for u in range(2):
                ln_lo(1, 0, u)
            split_weight_lo("w1b")
            gelu_split(1, 0, range(2))
            split_weight_lo("w2")
            gelu_split(1, 0, range(2, NM))
            split_weight_lo("wq")
            add1(0, 0)
            split_weight_lo("wk")
            add1(0, 1)
            split_weight_lo("wv")
            add1(0, 2)
            add1(0, 3)
            variance(2, 0)
            for t in range(NT):
                normal(2, 0, t)
            for u in range(2):
                ln_lo(2, 0, u)
            for tile in tiles[:2]:
                proj_lo(0, tile)
            e_id.wait(e, "dist")
            for b in B:
                more = b + 1 < NB
                attention(b)
                if more:
                    gelu_split(1, b + 1, range(EARLY, EARLY + 1))
                out_lo(b, 0)
                if more:
                    gelu_split(1, b + 1, range(EARLY + 1, EARLY + 2))
                out_lo(b, 1)
                out_lo(b, 2)
                if more:
                    gelu_split(1, b + 1, range(EARLY + 2, NM))
                add2(b, 0)
                out_lo(b, 3)
                add2(b, 1)
                add2(b, 2)
                add2(b, 3)
                variance(3, b)
                if more:
                    add1(b + 1, 0)
                normal(3, b, 0)
                normal(3, b, 1)
                if more:
                    add1(b + 1, 1)
                ln_lo(3, b, 0)
                normal(3, b, 2)
                normal(3, b, 3)
                if more:
                    add1(b + 1, 2)
                ln_lo(3, b, 1)
                if more:
                    add1(b + 1, 3)
                    variance(2, b + 1)
                gelu_split(2, b, range(2))
                if more:
                    normal(2, b + 1, 0)
                    normal(2, b + 1, 1)
                gelu_split(2, b, range(2, 5))
                if more:
                    normal(2, b + 1, 2)
                    normal(2, b + 1, 3)
                gelu_split(2, b, range(5, NM))
                if more:
                    ln_lo(2, b + 1, 0)
                    ln_lo(2, b + 1, 1)
                add3(b, 0)
                if more:
                    for tile in tiles[:2]:
                        proj_lo(b + 1, tile)
                add3(b, 1)
                add3(b, 2)
            add3(NB - 1, 3)

        @block.gpsimd
        def _(e):
            def power(L, b):
                e_ve.wait(e, (L, b))
                e_pw.by(e.tensor_tensor(rstd[:, L - 1, :], ve[:, L - 1, :], mhalf[:, :], ALU.pow), (L, b))

            def bias(L, b):
                e_xn.wait(e, (L, b, NT - 1))
                xs, bb = {1: (x0, b2h), 2: (x1, bo), 3: (x2, b2h)}[L]
                bb = bb[:, :].unsqueeze(1).broadcast_to([128, NT, D])
                e_pb.by(e.tensor_tensor(xs[:, :, :], xs[:, :, :], bb, ALU.add), (L, b))

            def attention(b):
                for s in range(H):
                    for i in QORDER:
                        e_rc.wait(e, (b, s, i // 2))
                        p = P[s % 2][:, QBASE[i]:QBASE[i] + 128 * (i + 1)]
                        e_nz.by(e.tensor_scalar(p, p, rs[:, s % 4, i:i + 1], 1.0, ALU.mult, ALU.mult), (b, s, i))
                    if b + 1 < NB:
                        if s == 12:
                            power(1, b + 1)
                        if s == 15:
                            bias(1, b + 1)

            e_id.by(e.memset(ident[:, :], 0.0), "zero")
            e_id.wait(e, "zero")
            e_id.by(e.affine_select(out=ident[:, :], in_=ident[:, :], compare_op=ALU.not_equal, fill=1.0,
                                    base=0, pattern=[[-1, 128]], channel_multiplier=1), "ident")
            e_id.by(e.iota(dist[:, :], [[1, T]], base=-(T - 128), channel_multiplier=-1,
                           allow_small_or_imprecise_dtypes=True), "iota")
            e_id.wait(e, "iota")
            e_id.by(e.affine_select(out=dist[:, :], in_=dist[:, :], compare_op=ALU.is_ge, fill=-BIG,
                                    base=T - 128, pattern=[[-1, T]], channel_multiplier=1), "dist")
            e_id.by(e.memset(mhalf[:, :], -0.5), "mhalf")
            e_id.wait(e, "mhalf")
            power(1, 0)
            e_w["b2"].wait(e, 0)
            e_sb.by(e.tensor_scalar(b2h[:, :], b2h[:, :], 0.5, 1.0, ALU.mult, ALU.mult), "b2")
            e_sb.wait(e, "b2")
            bias(1, 0)
            power(2, 0)
            e_w["bout"].wait(e, 0)
            bias(2, 0)
            for b in B:
                attention(b)
                power(3, b)
                bias(3, b)
                if b + 1 < NB:
                    power(2, b + 1)
                    bias(2, b + 1)


INPUTS = ["L0_attn_x", "L0_attn_w_qkv", "L0_attn_w_out", "L0_attn_b_out",
          "L0_ffn_w1", "L0_ffn_b1", "L0_ffn_w2", "L0_ffn_b2"]


def kernel(**inputs):
    import numpy as np
    import concourse.bacc as bacc
    from concourse import mybir
    from concourse.bass_utils import run_bass_kernel_spmd

    nc = bacc.Bacc("TRN2", target_bir_lowering=False, num_devices=1)
    arrays, args = {}, []
    for name in INPUTS:
        a = np.ascontiguousarray(inputs[name])
        arrays["in_" + name] = a
        args.append(nc.dram_tensor("in_" + name, a.shape, mybir.dt.from_np(a.dtype), kind="ExternalInput").ap())
    y = nc.dram_tensor("out_y", inputs["L0_attn_x"].shape, mybir.dt.float32, kind="ExternalOutput").ap()
    build(nc, *args, y)
    r = run_bass_kernel_spmd(nc, [arrays], core_ids=[0])
    return r.results[0]["out_y"]
```
